# Optimizing a Trainium2 kernel written in Bass

```python
import numpy as np
import jax
import jax.numpy as jnp

def _softmax(x, axis=-1):
    return jax.nn.softmax(x, axis=axis)

def _gelu(x):
    return jax.nn.gelu(x, approximate=True)

def _silu(x):
    return jax.nn.silu(x)

def _sigmoid(x):
    return jax.nn.sigmoid(x)

def _layernorm(x, axis=-1, eps=1e-05):
    m = jnp.mean(x, axis=axis, keepdims=True)
    v = jnp.var(x, axis=axis, keepdims=True)
    return (x - m) / jnp.sqrt(v + eps)

def _scatter_add(tgt, idx, src, axis=0):
    return tgt.at[idx].add(src)

def _segment_sum(src, seg, n):
    return jax.ops.segment_sum(src, seg, n)
kernel_name = 'mk_seq_postln_d1_jaxref_r8_28d2cb'

def setup_inputs(seed: int=0):
    np.random.seed(seed)
    _w = jnp.asarray

    def _L0_attn_setup():
        import jax, jax.numpy as jnp
        import numpy as np
        NUM_HEADS = 16
        D_MODEL = 128
        D_K = D_MODEL // NUM_HEADS
        MAX_SEQ_LEN = 512
        ROPE_BASE = 10000.0
        BATCH = 2
        SEQ_LEN = 256

        def _rope_tables(seq_len, d_k, base=ROPE_BASE):
            theta = 1.0 / base ** (jnp.arange(0, d_k, 2, dtype=jnp.float32) / d_k)
            m = jnp.arange(seq_len, dtype=jnp.float32)
            m_theta = jnp.outer(m, theta)
            ang = jnp.concatenate([m_theta, m_theta], axis=-1)
            return (jnp.cos(ang), jnp.sin(ang))

        def _apply_rope(x, cos, sin):
            d2 = x.shape[-1] // 2
            x1, x2 = (x[..., :d2], x[..., d2:])
            x_flip = jnp.concatenate([-x2, x1], axis=-1)
            return x * cos + x_flip * sin
        key = jax.random.key(seed)
        kx, kq, kk, kv, ko = jax.random.split(key, 5)
        s = 1.0 / np.sqrt(D_MODEL)
        x = jax.random.normal(kx, (BATCH, SEQ_LEN, D_MODEL), dtype=jnp.float32)
        W_Q = jax.random.uniform(kq, (D_MODEL, D_MODEL), jnp.float32, -s, s)
        W_K = jax.random.uniform(kk, (D_MODEL, D_MODEL), jnp.float32, -s, s)
        W_V = jax.random.uniform(kv, (D_MODEL, D_MODEL), jnp.float32, -s, s)
        W_O = jax.random.uniform(ko, (D_MODEL, D_MODEL), jnp.float32, -s, s)
        return {'x': x, 'W_Q': W_Q, 'W_K': W_K, 'W_V': W_V, 'W_O': W_O}
    _L0_attn_in = _L0_attn_setup()

    def _L0_ffn_setup():
        import jax, jax.numpy as jnp
        import numpy as np
        B, S, F, E, K = (4, 128, 128, 8, 2)
        H = 4 * F
        key = jax.random.key(seed)
        ks = jax.random.split(key, 7)

        def xavier(k, shape):
            fan_in, fan_out = (shape[-2], shape[-1])
            scale = jnp.sqrt(6.0 / (fan_in + fan_out))
            return jax.random.uniform(k, shape, jnp.float32, -scale, scale)
        return {'x': jax.random.normal(ks[0], (B, S, F), jnp.float32), 'Wg': xavier(ks[1], (F, E)), 'bg': jnp.zeros((E,), jnp.float32), 'W1': xavier(ks[2], (E, F, H)), 'b1': jnp.zeros((E, H), jnp.float32), 'W2': xavier(ks[3], (E, H, F)), 'b2': jnp.zeros((E, F), jnp.float32)}
    _L0_ffn_in = _L0_ffn_setup()
    _d = {'L0_attn_x': _L0_attn_in['x'], 'L0_attn_W_Q': _L0_attn_in['W_Q'], 'L0_attn_W_K': _L0_attn_in['W_K'], 'L0_attn_W_V': _L0_attn_in['W_V'], 'L0_attn_W_O': _L0_attn_in['W_O'], 'L0_ffn_Wg': _L0_ffn_in['Wg'], 'L0_ffn_bg': _L0_ffn_in['bg'], 'L0_ffn_W1': _L0_ffn_in['W1'], 'L0_ffn_b1': _L0_ffn_in['b1'], 'L0_ffn_W2': _L0_ffn_in['W2'], 'L0_ffn_b2': _L0_ffn_in['b2']}
    _x0 = _d['L0_attn_x']
    _d['L0_attn_x'] = jax.random.normal(jax.random.fold_in(jax.random.key(seed), 1), (4, 1024, 128), dtype=_x0.dtype)
    del _x0
    return _d

def reference(L0_attn_x, L0_attn_W_Q, L0_attn_W_K, L0_attn_W_V, L0_attn_W_O, L0_ffn_Wg, L0_ffn_bg, L0_ffn_W1, L0_ffn_b1, L0_ffn_W2, L0_ffn_b2):

    def _L0_attn_ref(x, W_Q, W_K, W_V, W_O):
        import jax, jax.numpy as jnp
        import numpy as np
        NUM_HEADS = 16
        D_MODEL = 128
        D_K = D_MODEL // NUM_HEADS
        MAX_SEQ_LEN = 512
        ROPE_BASE = 10000.0
        BATCH = 2
        SEQ_LEN = 256

        def _rope_tables(seq_len, d_k, base=ROPE_BASE):
            theta = 1.0 / base ** (jnp.arange(0, d_k, 2, dtype=jnp.float32) / d_k)
            m = jnp.arange(seq_len, dtype=jnp.float32)
            m_theta = jnp.outer(m, theta)
            ang = jnp.concatenate([m_theta, m_theta], axis=-1)
            return (jnp.cos(ang), jnp.sin(ang))

        def _apply_rope(x, cos, sin):
            d2 = x.shape[-1] // 2
            x1, x2 = (x[..., :d2], x[..., d2:])
            x_flip = jnp.concatenate([-x2, x1], axis=-1)
            return x * cos + x_flip * sin
        B, S, _ = x.shape

        def proj(W):
            y = jnp.einsum('bsd,ed->bse', x, W)
            return y.reshape(B, S, NUM_HEADS, D_K).transpose(0, 2, 1, 3)
        Q, K, V = (proj(W_Q), proj(W_K), proj(W_V))
        cos, sin = _rope_tables(S, D_K)
        Q = _apply_rope(Q, cos, sin)
        K = _apply_rope(K, cos, sin)
        scores = jnp.einsum('bhsd,bhtd->bhst', Q, K) / jnp.sqrt(jnp.float32(D_K))
        causal = jnp.tril(jnp.ones((S, S), dtype=bool))
        scores = jnp.where(causal[None, None], scores, -jnp.inf)
        attn = jax.nn.softmax(scores, axis=-1)
        out = jnp.einsum('bhst,bhtd->bhsd', attn, V)
        out = out.transpose(0, 2, 1, 3).reshape(B, S, D_MODEL)
        return jnp.einsum('bsd,ed->bse', out, W_O)

    def _L0_ffn_ref(x, Wg, bg, W1, b1, W2, b2):
        import jax, jax.numpy as jnp
        import numpy as np
        B, S, F, E, K = (4, 128, 128, 8, 2)
        H = 4 * F
        gate_probs = jax.nn.softmax(x @ Wg + bg, axis=-1)
        k = K
        _, top_idx = jax.lax.top_k(gate_probs, k)
        expert_mask = jax.nn.one_hot(top_idx, gate_probs.shape[-1], dtype=gate_probs.dtype).sum(-2)
        selected = gate_probs * expert_mask
        selected = selected / (selected.sum(-1, keepdims=True) + 1e-08)
        h = jax.nn.gelu(jnp.einsum('bsf,efh->bseh', x, W1) + b1)
        expert_out = jnp.einsum('bseh,ehf->bsef', h, W2) + b2[None, None]
        return jnp.einsum('bsef,bse->bsf', expert_out, selected)
    x = L0_attn_x
    x = _layernorm(x + _L0_attn_ref(x, L0_attn_W_Q, L0_attn_W_K, L0_attn_W_V, L0_attn_W_O), axis=-1)
    x = _layernorm(x + _L0_ffn_ref(x, L0_ffn_Wg, L0_ffn_bg, L0_ffn_W1, L0_ffn_b1, L0_ffn_W2, L0_ffn_b2), axis=-1)
    return x

_drawn_inputs = setup_inputs


def setup_inputs(seed=0):
    import zlib

    import numpy as np

    out = dict(_drawn_inputs(seed))
    spreads = {'L0_ffn_bg': (0.0, 0.1), 'L0_ffn_b1': (0.0, 0.1), 'L0_ffn_b2': (0.0, 0.1)}
    factors = {}
    for name, (base, spread) in spreads.items():
        noise = np.random.default_rng([zlib.crc32(name.encode()), seed]).standard_normal(out[name].shape)
        drawn = base * np.exp(spread * noise) if base else spread * noise
        out[name] = jnp.asarray(drawn.astype(out[name].dtype))
    for name, factor in factors.items():
        out[name] = (out[name] * factor).astype(out[name].dtype)
    return out
```

```python
from contextlib import ExitStack

import numpy as np
import concourse.bass as bass
from concourse import mybir

F32 = mybir.dt.float32
BF16 = mybir.dt.bfloat16
ALU = mybir.AluOpType
ACT = mybir.ActivationFunctionType
AX = mybir.AxisListType

P = 128
B, S, D = 4, 1024, 128
H, DK = 16, 8
E, HID = 8, 512
NT = B * S // P
BT = S // P
GH = 4
NG = H // GH
CH = 512
NCH = B * S // CH
HC = HID // P
ROWS = 56
MROW = 32
Q_PARTS = ((0, 0), (8, 0), (16, 1), (24, 1), (40, 0), (48, 2))
K_PARTS = ((0, 0), (8, 1), (16, 0), (24, 1), (40, 2), (48, 0))
SCALE = float(np.float32(1.0) / np.sqrt(np.float32(DK)))
EPS = 1e-5
GATE_EPS = 1e-8
RING = 3


def pass_a_items():
    items = []
    for sb in range(BT):
        whole, rest = divmod((sb + 1) * P, CH)
        parts = [(CH * i, CH) for i in range(whole)] + ([(CH * whole, rest)] if rest else [])
        for t0, n in parts:
            masked = t0 + n == (sb + 1) * P
            if 2 * n <= CH:
                items += [(par, sb, t0, n, (0, 1), masked) for par in (0, 1)]
            else:
                items += [(par, sb, t0, n, (slot,), masked) for slot in (0, 1) for par in (0, 1)]
    return items


def pass_b_steps():
    steps = []
    for c in range(S // CH):
        for j in range((c + 1) * CH // P):
            s0 = max(P * j, CH * c)
            steps.append((c, j, s0, CH * (c + 1) - s0))
    return steps


A_ITEMS = pass_a_items()
B_STEPS = pass_b_steps()
NA, NB = len(A_ITEMS), len(B_STEPS)
C_LAST = [max(k for k, st in enumerate(B_STEPS) if st[0] == c) for c in range(2)]


def split_items():
    out = [list(A_ITEMS) for _ in range(NG)]
    g = 0
    while (sum(len(o) for o in out) + NG * 3) % RING:
        i = next(i for i, it in enumerate(out[g]) if len(it[4]) == 2)
        par, sb, t0, n, slots, masked = out[g][i]
        out[g][i:i + 1] = [(par, sb, t0, n, (s,), masked) for s in slots]
    return out


A_OF = split_items()


def unit_plan(g, with_a):
    nxt = (g + 1) % NG
    a = list(A_OF[nxt]) if with_a else []
    plan = []
    total = len(a)
    done = 0

    def take(upto):
        nonlocal done
        while done < min(upto, total):
            plan.append(("A", nxt, a[done]))
            done += 1

    take(8)
    plan.append(("QK", 0))
    for k in range(NB):
        if k + 1 < NB:
            plan.append(("QK", k + 1))
        take(8 + (total - 8) * (k + 1) // (NB - 2))
        plan.append(("PV", k))
        if k == C_LAST[0] + 2:
            plan.append(("OT", 0))
        if k == NB - 2 and with_a:
            plan.append(("MT", nxt))
    plan.append(("OT", 1))
    return plan


PROLOGUE = [("A", 0, it) for it in A_OF[0]] + [("MT", 0)]
RING_PRO = len(PROLOGUE)


def batch_plan(last):
    plan, k = [], 0
    for g in range(NG):
        unit = []
        for step in unit_plan(g, not (last and g == NG - 1)):
            if step[0] in ("A", "MT", "OT"):
                unit.append((step, k))
                k += 1
            else:
                unit.append((step, None))
        plan.append(unit)
    return plan, k


RING_BATCH = batch_plan(False)[1]
assert RING_BATCH % RING == 0


def build(nc, xT, x, wqT, wqfT, wkT, wkfT, wvT, woT, wg, bg, w1, b1T, w2, b2,
          cosT, sinT, ident, maskA, maskB, out):
    ctx = ExitStack()
    with ctx:
        def sb(name, shape, dt=F32):
            return ctx.enter_context(nc.sbuf_tensor(name, shape, dt))

        def sem(name):
            return ctx.enter_context(nc.semaphore(name))

        stack = nc.dram_tensor("stack", [2, B, H, 64, S], BF16, kind="Internal").ap()

        xT_sb = sb("xT_sb", [P, B * S])
        x_sb = sb("x_sb", [P, NT, D])
        w_sb = sb("w_sb", [P, 6, D])
        wg_sb = sb("wg_sb", [P, E])
        bg_sb = sb("bg_sb", [P, E])
        w1_sb = sb("w1_sb", [P, E, HID])
        b1_sb = sb("b1_sb", [P, E * HC])
        w2_sb = sb("w2_sb", [P, E, HC, D])
        b2_sb = sb("b2_sb", [P, E, D])
        cs_sb = sb("cs_sb", [P, 2, S])
        id_sb = sb("id_sb", [P, P])
        idb_sb = sb("idb_sb", [P, P], BF16)
        mask_sb = sb("mask_sb", [P, 2, 2, P], BF16)
        mask_f = sb("mask_f", [P, 2, P])
        fill = sb("fill", [H, 2, S], BF16)
        v_sb = sb("v_sb", [P, NT, D])
        attn = sb("attn", [P, NT, D])
        region = sb("region", [P, 16384])
        logits = sb("logits", [P, NT, E])
        gates = sb("gates", [P, NT, E])
        rt = sb("rt", [P, 8, NT, E])
        r1 = sb("r1", [P, 8, NT])
        iota_e = sb("iota_e", [P, E])

        rot = region[:, 0:2 * 2048].rearrange("p (b t w n) -> p b t w n", b=2, t=2, w=2)
        rem = region[:, 4096:4096 + 2 * 2048].rearrange("p (b t w n) -> p b t w n", b=2, t=2, w=2)
        parts = region[:, 8192:8192 + 3072].bitcast(BF16).rearrange(
            "p (b j w n) -> p b j w n", b=2, j=3, w=2)
        qst = region[:, 0:4096].bitcast(BF16).rearrange("p (g s n) -> p g s n", g=NG, s=2)
        kst = region[:, 4096:8192].bitcast(BF16).rearrange("p (g s n) -> p g s n", g=NG, s=2)
        probs = region[:, 8192:12288].rearrange("p (k w n) -> p k w n", k=4, w=2)
        vx = region[:, 12288:16384].rearrange("p (g t h c) -> p g t h c", g=NG, t=BT, h=GH)
        ot = sb("ot", [P, 2, CH])
        rden = sb("rden", [P, 2, 4 * GH])
        mx = sb("mx", [P, 2, GH, BT])
        mx2 = sb("mx2", [P, 2, GH, BT // 2])
        mrem = sb("mrem", [P, 2, GH, BT])
        zero = sb("zero", [P, GH, BT])
        msp = sb("msp", [P, 2, GH, 3, BT], BF16)
        mparts = sb("mparts", [GH * 3 * BT, 2, P], BF16)
        stg = region[:, 0:1024].rearrange("p (b t n) -> p b t n", b=2, t=4)
        aT = region[:, 1024:2048].rearrange("p (b n) -> p b n", b=2)
        y1 = region[:, 2048:3072].rearrange("p (b t n) -> p b t n", b=2, t=4)
        x1T = region[:, 3072:4096].rearrange("p (b n) -> p b n", b=2)
        x1s = region[:, 4096:5120].rearrange("p (b t n) -> p b t n", b=2, t=4)
        hT = region[:, 5120:6144].rearrange("p (b n) -> p b n", b=2)
        acc = region[:, 6144:7168].rearrange("p (b t n) -> p b t n", b=2, t=4)
        yb = region[:, 7168:8192].rearrange("p (b t n) -> p b t n", b=2, t=4)
        fin = region[:, 8192:9216].rearrange("p (b t n) -> p b t n", b=2, t=4)
        stats = sb("stats", [P, 2, 4, 6])
        mean = sb("mean", [P, 2, 4])
        dev = sb("dev", [P, 2, 3, 4])
        std = sb("std", [P, 2, 4])
        rstd = sb("rstd", [P, 2, 4])
        stats_all = sb("stats_all", [P, NT, 6])
        mean_all = sb("mean_all", [P, NT])
        dev_all = sb("dev_all", [P, 3, NT])
        std_all = sb("std_all", [P, NT])
        rstd_all = sb("rstd_all", [P, NT])
        eps_sb = sb("eps_sb", [P, 1])

        banks = ctx.enter_context(nc.psum_tensor("banks", [P, 8, CH], F32))
        ring = banks[:, 0:RING, :]
        score = banks[:, RING:RING + 4, :].rearrange("p (k w) n -> p k w n", k=2)
        pv = banks[:, RING + 4, :]

        loads = sem("loads")
        fill_set = sem("fill_set")
        masks_ready = sem("masks_ready")
        fills = sem("fills")
        proj_done = sem("proj_done")
        proj_read = sem("proj_read")
        rotated = sem("rotated")
        part_done = sem("part_done")
        rem_done = sem("rem_done")
        stored = [sem(f"stored{i}") for i in range(2)]
        v_done = sem("v_done")
        v_read = sem("v_read")
        vx_set = sem("vx_set")
        dma_unit = [sem(f"unit_loaded{g}") for g in range(NG)]
        vx_ready = sem("vx_ready")
        ring_full = sem("ring_full")
        ring_read = sem("ring_read")
        mx_ready = sem("mx_ready")
        msplit = sem("msplit")
        mrows = [sem(f"mrows{i}") for i in range(2)]
        qk_done = sem("qk_done")
        exp_done = sem("exp_done")
        pv_done = sem("pv_done")
        ot_ready = sem("ot_ready")
        ot_used = sem("ot_used")
        dve = sem("dve")
        attn_done = sem("attn_done")
        staged = [sem(f"staged{i}") for i in range(2)]
        t1_done = sem("t1_done")
        aT_ready = sem("aT_ready")
        wo_done = sem("wo_done")
        x1_done = sem("x1_done")
        t2_done = sem("t2_done")
        x1T_ready = sem("x1T_ready")
        lg_done = sem("lg_done")
        lg_read = sem("lg_read")
        iota_done = sem("iota_done")
        top_in = sem("top_in")
        staged2 = sem("logits_kept")
        top_exp = sem("top_exp")
        gates_done = sem("gates_done")
        h_done = sem("h_done")
        gelu_done = sem("gelu_done")
        y_done = sem("y_done")
        y_used = sem("y_used")
        fin_ready = sem("fin_ready")
        var_done = sem("var_done")
        std_done = sem("std_done")
        var2_done = sem("var2_done")
        std2_done = sem("std2_done")
        out_done = sem("out_done")

        N_LOADS = 19
        block = ctx.enter_context(nc.Block())

        @block.sync
        def _(sp):
            wlist = [wqT, wqfT, wkT, wkfT, wvT, woT]
            for i, w in enumerate(wlist):
                sp.dma_start(w_sb[:, i, :], w).then_inc(loads, 16)
            sp.dma_start(xT_sb[:, :], xT).then_inc(loads, 16)
            sp.dma_start(cs_sb[:, 0, :], cosT).then_inc(loads, 16)
            sp.dma_start(cs_sb[:, 1, :], sinT).then_inc(loads, 16)
            sp.dma_start(id_sb[:, :], ident).then_inc(loads, 16)
            sp.dma_start(mask_f[:, 0, :], maskA).then_inc(loads, 16)
            sp.dma_start(mask_f[:, 1, :], maskB).then_inc(loads, 16)
            sp.dma_start(wg_sb[:, :], wg).then_inc(loads, 16)
            sp.dma_start(bg_sb[:, :], bg.partition_broadcast(P)).then_inc(loads, 16)
            sp.dma_start(b1_sb[:, :], b1T).then_inc(loads, 16)
            sp.dma_start(b2_sb[:, :, :], b2.partition_broadcast(P)).then_inc(loads, 16)
            sp.dma_start(x_sb[:, :, :], x.rearrange("(t p) n -> p t n", p=P)).then_inc(loads, 16)
            sp.dma_start(w1_sb[:, :, :], w1.rearrange("e p n -> p e n")).then_inc(loads, 16)
            sp.dma_start(w2_sb[:, :, :, :], w2.rearrange("e (c p) n -> p e c n", p=P)).then_inc(loads, 16)
            sp.wait_ge(fill_set, 2)
            for w, row, n, one in ((0, MROW, 8, 0), (1, MROW, 3, 1), (1, MROW + 3, 5, 0)):
                for b in range(B):
                    sp.dma_start(stack[w, b, :, row:row + n, :],
                                 fill[:, one:one + 1, :].broadcast_to([H, n, S])).then_inc(fills, 16)

            def store(c, i):
                b, half = c // 2, i
                sp.wait_ge(rem_done, 2 * (c + 1))
                for w, plan in ((0, Q_PARTS), (1, K_PARTS)):
                    for row, part in plan:
                        sp.dma_start(stack[w, b, :, row:row + 8, half * CH:(half + 1) * CH],
                                     parts[:, i, part, w, :]).then_inc(stored[i], 16)

            for c in range(NCH):
                store(c, c % 2)
            sp.wait_ge(fills, 16 * 3 * B)
            for i in range(2):
                sp.wait_ge(stored[i], 16 * 12 * (NCH // 2))
            sp.wait_ge(v_read, NT // 4)

            def load_unit(b, g):
                for w, dst in ((0, qst), (1, kst)):
                    for par in (0, 1):
                        src = stack[w, bass.ds(b, 1), GH * g + par:GH * g + par + 3:2, 0:ROWS, :]
                        sp.dma_start(dst[64 * par:64 * par + ROWS, g, :, :],
                                     src.rearrange("o s r n -> (o r) s n")).then_inc(dma_unit[g], 16)

            def m_rows(g, at):
                if at is None:
                    sp.wait_ge(ring_read, RING_PRO)
                else:
                    sp.wait_ge(ring_read, at)
                for h in range(GH):
                    sp.dma_start(qst[64 * (h % 2) + MROW:64 * (h % 2) + MROW + 3, g, h // 2, :],
                                 mparts[h * 3 * BT:(h + 1) * 3 * BT, g % 2, :]).then_inc(mrows[g % 2], 16)

            load_unit(0, 0)
            load_unit(0, 1)
            load_unit(0, 2)
            m_rows(0, None)

            def batch(b, last):
                plan = batch_plan(last)[0]
                for g in range(NG):
                    if not (last and g > 0):
                        sp.wait_ge(qk_done, b * (NG * NB * 2) + g * NB * 2 + 1)
                        load_unit(b + (g + 3) // NG, (g + 3) % NG)
                    if not (last and g == NG - 1):
                        r = next(r for s, r in plan[g] if s[0] == "MT")
                        m_rows((g + 1) % NG, b * RING_BATCH + (RING_PRO + r + 1))

            with sp.Fori(0, B - 1) as b:
                batch(b, False)
            batch(B - 1, True)

            sp.wait_ge(attn_done, 1)
            sp.dma_start(stg[:, 0, :, :], attn[:, 0:4, :]).then_inc(staged[0], 16)
            sp.dma_start(stg[:, 1, :, :], attn[:, 4:8, :]).then_inc(staged[1], 16)
            with sp.Fori(0, NCH // 2 - 1) as i:
                for k in range(2):
                    sp.wait_ge(t1_done, i * 2 + (k + 1))
                    sp.dma_start(stg[:, k, :, :], attn[:, bass.ds(i * 8 + (4 * k + 8), 4), :]).then_inc(staged[k], 16)

            for b in range(B):
                sp.wait_ge(fin_ready, b + 1)
                sp.dma_start(out.rearrange("(b t p) n -> b p t n", b=B, p=P)[b], x_sb[:, b * BT:(b + 1) * BT, :]
                             ).then_inc(out_done, 16)
            sp.wait_ge(out_done, 16 * B)

        @block.tensor
        def _(pe):
            pe.sem_inc(qk_done, 1)
            pe.sem_inc(pv_done, 1)
            mm = nc.tensor.matmul
            pe.wait_ge(loads, 16 * N_LOADS)
            for c in range(NCH):
                bank = 4 * (c % 2)
                if c >= 2:
                    pe.wait_ge(proj_read, c - 1)
                for i, w in enumerate((0, 2, 1, 3)):
                    last = mm(banks[:, bank + i, :], w_sb[:, w, :], xT_sb[:, c * CH:(c + 1) * CH],
                              start=True, stop=True)
                last.then_inc(proj_done, 1)
            pe.wait_ge(proj_read, NCH)
            for c in range(NT // 4):
                if c >= 8:
                    pe.wait_ge(v_read, c - 7)
                for t in range(4):
                    tile = 4 * c + t
                    last = mm(banks[:, c % 8, t * P:(t + 1) * P], xT_sb[:, tile * P:(tile + 1) * P],
                              w_sb[:, 4, :], start=(t == 0), stop=True, skip_group_check=True)
                last.then_inc(v_done, 1)
            pe.wait_ge(v_read, NT // 4)

            pe.wait_ge(masks_ready, 2)

            def ring_wait(k, at):
                if isinstance(k, int) and k < RING:
                    return
                pe.wait_ge(ring_read, k - RING + 1)

            def pass_a(g, item, bank):
                par, sb_, t0, n, slots, masked = item
                rows = slice(64 * par, 64 * par + ROWS)
                for i, slot in enumerate(slots):
                    last = mm(ring[:, bank, i * n:(i + 1) * n], qst[rows, g, slot, sb_ * P:(sb_ + 1) * P],
                              kst[rows, g, slot, t0:t0 + n], start=(i == 0), stop=not masked,
                              skip_group_check=True)
                if masked:
                    k = len(slots)
                    view = ring[:, bank, 0:k * n].rearrange("p (k n) -> p k n", k=k)[:, :, n - P:n]
                    last = mm(view, idb_sb[:, :], mask_sb[:, 0, 0:k, :], start=False, stop=True,
                              skip_group_check=True)
                last.then_inc(ring_full, 1)

            def pe_ring(step, k, at):
                ring_wait(k, at)
                bank = at % RING
                if step[0] == "A":
                    pass_a(step[1], step[2], bank)
                elif step[0] == "MT":
                    nc.tensor.transpose(ring[0:GH * 3 * BT, bank, 0:P // 2].bitcast(BF16),
                                        msp[:, step[1] % 2, :, :, :].rearrange("p h j s -> p (h j s)"),
                                        idb_sb[:, :]).then_inc(ring_full, 1)
                else:
                    c = step[1]
                    for t in range(4):
                        last = nc.tensor.transpose(ring[:, bank, t * P:(t + 1) * P],
                                                   ot[:, c, t * P:(t + 1) * P], id_sb[:, :])
                    last.then_inc(ring_full, 1)

            pe.wait_ge(dma_unit[0], 64)
            for k, step in enumerate(PROLOGUE):
                if step[0] == "MT":
                    pe.wait_ge(msplit, 4)
                pe_ring(step, k, k)

            def batch(b, last):
                for g, unit in enumerate(batch_plan(last)[0]):
                    u = b * NG + g
                    first = True
                    for step, r in unit:
                        if step[0] == "A" and first:
                            pe.wait_ge(dma_unit[(g + 1) % NG], 64 * (b + (g + 1) // NG) + 64)
                            first = False
                        if step[0] == "MT":
                            pe.wait_ge(msplit, u * 4 + 8)
                        if step[0] == "OT":
                            pe.wait_ge(ot_ready, u * 2 + step[1] + 1 + 1)
                        if r is not None:
                            pe_ring(step, b * RING_BATCH + (RING_PRO + r), RING_PRO + r)
                            if step[0] == "OT":
                                pass
                        elif step[0] == "QK":
                            k = step[1]
                            c, j, s0, n = B_STEPS[k]
                            if k == 0:
                                pe.wait_ge(mrows[g % 2], b * 128 + ((g // 2) * 64 + 64))
                            for slot in (0, 1):
                                i = 2 * k + slot
                                if k == 0 and g == 0 and isinstance(b, int) and b == 0:
                                    pass
                                elif k == 0 and g == 0:
                                    pe.wait_ge(exp_done, b * (NG * NB * 2) + 1)
                                else:
                                    pe.wait_ge(exp_done, u * (2 * NB) + (i - 1) + 1)
                                for par in (0, 1):
                                    rows = slice(64 * par, 64 * par + ROWS)
                                    last_mm = mm(score[:, slot, par, 0:n],
                                                 kst[rows, g, slot, j * P:(j + 1) * P],
                                                 qst[rows, g, slot, s0:s0 + n], start=True,
                                                 stop=(s0 != j * P), skip_group_check=True)
                                if s0 == j * P:
                                    for par in (0, 1):
                                        last_mm = mm(score[:, slot, par, 0:P], idb_sb[:, :],
                                                     mask_sb[:, 1, 0, :], start=False, stop=True,
                                                     skip_group_check=True)
                                last_mm.then_inc(qk_done, 1)
                        else:
                            k = step[1]
                            c, j, s0, n = B_STEPS[k]
                            if k == 0:
                                pe.wait_ge(vx_ready, u + 1)
                            if j == 0:
                                pe.wait_ge(ot_ready, u * 2 + c + 1)
                            pe.wait_ge(exp_done, u * (2 * NB) + (2 * k + 2) + 1)
                            for slot in (0, 1):
                                for par in (0, 1):
                                    h = 2 * slot + par
                                    last_mm = mm(pv[32 * h:32 * h + 32, s0 - c * CH:s0 - c * CH + n],
                                                 vx[:, g, j, h, :], probs[:, (2 * k + slot) % 4, par, 0:n],
                                                 start=(j == 0), stop=(k == C_LAST[c]),
                                                 tile_position=(0, 32 * h), skip_group_check=True)
                            last_mm.then_inc(pv_done, 1)

            with pe.Fori(0, B - 1) as b:
                batch(b, False)
            batch(B - 1, True)

            pe.wait_ge(attn_done, 1)
            with pe.Fori(0, NCH // 2) as i:
                for k in range(2):
                    n = i * 2 + k
                    pe.wait_ge(staged[k], i * 16 + 16)
                    for t in range(4):
                        last = nc.tensor.transpose(banks[:, k, t * P:(t + 1) * P], stg[:, k, t, :], id_sb[:, :])
                    last.then_inc(t1_done, 1)
                    pe.wait_ge(aT_ready, n + 1)
                    for t in range(4):
                        last = mm(banks[:, 2 + k, t * P:(t + 1) * P], aT[:, k, t * P:(t + 1) * P], w_sb[:, 5, :],
                                  start=(t == 0), stop=True, skip_group_check=True)
                    last.then_inc(wo_done, 1)
                    pe.wait_ge(x1_done, n + 1)
                    for t in range(4):
                        last = nc.tensor.transpose(banks[:, 4 + k, t * P:(t + 1) * P], x1s[:, k, t, :], id_sb[:, :])
                    last.then_inc(t2_done, 1)
                    pe.wait_ge(x1T_ready, n + 1)
                    for t in range(4):
                        last = mm(banks[:, 6 + k, t * E:(t + 1) * E], x1T[:, k, t * P:(t + 1) * P], wg_sb[:, :],
                                  start=(t == 0), stop=True, skip_group_check=True)
                    last.then_inc(lg_done, 1)
                    pe.wait_ge(lg_read, n + 1)

            with pe.Fori(0, NCH) as i:
                pe.wait_ge(lg_read, NCH)

                def up(q):
                    e, hc = divmod(q, HC)
                    if q >= 2:
                        pe.wait_ge(gelu_done, i * (E * HC) + (q - 1) + 1)
                    else:
                        pe.wait_ge(gelu_done, i * (E * HC) + 1)
                    mm(banks[:, q % 2, :], w1_sb[:, e, hc * P:(hc + 1) * P], xT_sb[:, bass.ts(i, CH)],
                       start=True, stop=True).then_inc(h_done, 1)

                up(0)
                for q in range(E * HC):
                    e, hc = divmod(q, HC)
                    if q + 1 < E * HC:
                        up(q + 1)
                    pe.wait_ge(gelu_done, i * (E * HC) + (q + 1) + 1)
                    if hc == 0:
                        if e >= 2:
                            pe.wait_ge(y_used, i * E + (e - 1) + 1)
                        else:
                            pe.wait_ge(y_used, i * E + 1)
                    for t in range(4):
                        last = mm(banks[:, 2 + e % 2, t * P:(t + 1) * P], hT[:, q % 2, t * P:(t + 1) * P],
                                  w2_sb[:, e, hc, :], start=(hc == 0 and t == 0), stop=(hc == HC - 1),
                                  skip_group_check=True)
                    if hc == HC - 1:
                        last.then_inc(y_done, 1)

        @block.scalar
        def _(act):
            act.sem_inc(exp_done, 1)
            act.sem_inc(ot_ready, 1)
            act.sem_inc(gelu_done, 1)
            for c in range(NCH):
                i = c % 2
                for j in range(2):
                    if j == 0:
                        act.wait_ge(rotated, c + 1)
                        if c >= 2:
                            act.wait_ge(stored[i], 16 * 12 * (c // 2))
                    else:
                        act.wait_ge(rem_done, 2 * c + 1)
                    nc.scalar.copy(parts[:, i, j, :, :], rem[:, i, 0, :, :] if j == 0 else rem[:, i, 1, :, :]
                                   ).then_inc(part_done, 1)

            def batch(b, last):
                for g in range(NG):
                    u = b * NG + g
                    for k in range(NB):
                        c, j, s0, n = B_STEPS[k]
                        for slot in (0, 1):
                            i = 2 * k + slot
                            act.wait_ge(qk_done, u * (2 * NB) + (i + 1) + 1)
                            if not (isinstance(b, int) and b == 0 and g == 0 and k < 2):
                                if g == 0 and k < 2:
                                    act.wait_ge(pv_done, b * (NG * NB) + 1)
                                else:
                                    act.wait_ge(pv_done, u * NB + (k - 1) + 1)
                            nc.scalar.activation(probs[:, i % 4, :, 0:n], score[:, slot, :, 0:n], ACT.Exp,
                                                 scale=SCALE).then_inc(exp_done, 1)
                        if k - 1 == C_LAST[0]:
                            empty(b, g, 0)
                    empty(b, g, 1)

            def empty(b, g, c):
                u = b * NG + g
                act.wait_ge(pv_done, u * NB + (C_LAST[c] + 1) + 1)
                act.wait_ge(ot_used, u * 2 + 1)
                nc.scalar.copy(ot[:, c, :], pv[:, :]).then_inc(ot_ready, 1)

            with act.Fori(0, B - 1) as b:
                batch(b, False)
            batch(B - 1, True)

            act.wait_ge(iota_done, 1)
            with act.Fori(0, NCH // 2) as i:
                for k in range(2):
                    n = i * 2 + k
                    act.wait_ge(t1_done, n + 1)
                    nc.scalar.copy(aT[:, k, :], banks[:, k, :]).then_inc(aT_ready, 1)
                    act.wait_ge(var_done, n + 1)
                    nc.scalar.activation(std[:, k, :], dev[:, k, 0, :], ACT.Sqrt, bias=eps_sb[:, :], scale=1.0 / D).then_inc(std_done, 1)
                    act.wait_ge(t2_done, n + 1)
                    nc.scalar.copy(x1T[:, k, :], banks[:, 4 + k, :]).then_inc(x1T_ready, 1)
                    act.wait_ge(x1T_ready, n + 1)
                    nc.scalar.copy(xT_sb[:, bass.ts(n, CH)], x1T[:, k, :]).then_inc(lg_read, 1)

            act.wait_ge(top_in, 1)
            nc.scalar.activation(rt[:, 1, :, :], rt[:, 0, :, :], ACT.Exp).then_inc(top_exp, 1)

            with act.Fori(0, NCH) as i:
                for q in range(E * HC):
                    act.wait_ge(h_done, i * (E * HC) + (q + 1))
                    e, hc = divmod(q, HC)
                    nc.scalar.activation(hT[:, q % 2, :], banks[:, q % 2, :], ACT.Gelu_apprx_tanh,
                                         bias=b1_sb[:, q:q + 1]).then_inc(gelu_done, 1)
            act.wait_ge(var2_done, 1)
            nc.scalar.activation(std_all[:, :], dev_all[:, 0, :], ACT.Sqrt, bias=eps_sb[:, :], scale=1.0 / D).then_inc(std2_done, 1)

        @block.vector
        def _(ve):
            ve.sem_inc(ot_used, 1)
            ve.sem_inc(y_used, 1)
            v = nc.vector
            link = [0]

            def chain(ins):
                link[0] += 1
                ins.then_inc(dve, 1)
                ve.wait_ge(dve, link[0])

            ve.wait_ge(loads, 16 * N_LOADS)
            v.tensor_copy(idb_sb[:, :], id_sb[:, :]).then_inc(masks_ready, 1)
            v.tensor_copy(mask_sb[:, :, :, :], mask_f[:, :, :].unsqueeze(2).broadcast_to([P, 2, 2, P])
                          ).then_inc(masks_ready, 1)
            for c in range(NCH):
                i = c % 2
                h = c % 2
                bank = 4 * i
                ve.wait_ge(proj_done, c + 1)
                if c >= 2:
                    ve.wait_ge(rem_done, 2 * (c - 1))
                cos = cs_sb[:, 0, h * CH:(h + 1) * CH].unsqueeze(1).broadcast_to([P, 2, CH])
                sin = cs_sb[:, 1, h * CH:(h + 1) * CH].unsqueeze(1).broadcast_to([P, 2, CH])
                v.tensor_tensor(rot[:, i, 0, :, :], banks[:, bank:bank + 2, :], cos, ALU.mult).then_inc(dve, 1)
                link[0] += 1
                v.tensor_tensor(rot[:, i, 1, :, :], banks[:, bank + 2:bank + 4, :], sin,
                                ALU.mult).then_inc(proj_read, 1)
                ve.wait_ge(dve, link[0])
                ve.wait_ge(proj_read, c + 1)
                v.tensor_tensor(rem[:, i, 0, :, :], rot[:, i, 0, :, :], rot[:, i, 1, :, :],
                                ALU.add).then_inc(rotated, 1)
            for c in range(NT // 4):
                ve.wait_ge(v_done, c + 1)
                v.tensor_copy(v_sb[:, 4 * c:4 * c + 4, :],
                              banks[:, c % 8, :].rearrange("p (t n) -> p t n", t=4)).then_inc(v_read, 1)

            NCHAIN = 0

            def reduce_item(g, item, bank):
                par, sb_, t0, n, slots, masked = item
                hs = slice(2 * slots[0] + par, 2 * slots[-1] + par + 1, 2)
                dst = mx[:, g % 2, hs, sb_] if t0 == 0 else mx2[:, g % 2, hs, sb_ - BT // 2]
                src = ring[:, bank, 0:len(slots) * n].rearrange("p (k n) -> p k n", k=len(slots))
                v.tensor_reduce(dst, src, AX.X, ALU.max, negate=True).then_inc(ring_read, 1)


            def dve_ring(step, k, at, u):
                bank = at % RING
                ve.wait_ge(ring_full, k + 1)
                if step[0] == "A":
                    reduce_item(step[1], step[2], bank)
                elif step[0] == "MT":
                    v.tensor_copy(mparts[:, step[1] % 2, :],
                                  ring[0:GH * 3 * BT, bank, 0:P // 2].bitcast(BF16)).then_inc(ring_read, 1)
                else:
                    c = step[1]
                    view = ring[:, bank, :].rearrange("p (t h d) -> p t h d", t=4, h=GH)
                    v.reciprocal(rden[:, c, :].rearrange("p (t h) -> p t h", t=4),
                                 view[:, :, :, DK]).then_inc(ot_used, 1)
                    b, g = u
                    ve.wait_ge(ot_used, (b * NG + g) * 2 + (c + 1) + 1)
                    tile = b * BT + c * 4
                    v.tensor_tensor(attn[:, bass.ds(tile, 4), g * 32:(g + 1) * 32].rearrange(
                                        "p t (h d) -> p t h d", h=GH),
                                    view[:, :, :, 0:DK],
                                    rden[:, c, :].rearrange("p (t h) -> p t h", t=4).unsqueeze(3).broadcast_to(
                                        [P, 4, GH, DK]), ALU.mult).then_inc(ring_read, 1)

            def finish_max(g, k, unit):
                ve.wait_ge(ring_read, k + 1)
                v.tensor_tensor(mx[:, g % 2, :, BT // 2:BT], mx[:, g % 2, :, BT // 2:BT], mx2[:, g % 2, :, :],
                                ALU.min).then_inc(mx_ready, 1)

            na0 = len(A_OF[0])
            for k, step in enumerate(PROLOGUE):
                if step[0] == "A":
                    dve_ring(step, k, k, None)
                    if k == na0 - 1:
                        finish_max(0, k, 0)
                else:
                    dve_ring(step, k, k, None)

            def batch(b, last):
                for g, unit in enumerate(batch_plan(last)[0]):
                    left = sum(1 for s, r in unit if s[0] == "A")
                    for step, r in unit:
                        if r is None:
                            continue
                        if step[0] == "A" and left == len(A_OF[(g + 1) % NG]):
                            pass
                        if step[0] == "MT":
                            pass
                        k = b * RING_BATCH + (RING_PRO + r)
                        dve_ring(step, k, RING_PRO + r, (b, g))
                        if step[0] == "A":
                            left -= 1
                            if left == 0:
                                finish_max((g + 1) % NG, k, b * NG + g + 1)

            with ve.Fori(0, B - 1) as b:
                batch(b, False)
            batch(B - 1, True)
            ring_total = RING_PRO + B * RING_BATCH - len(A_OF[0]) - 1
            ve.wait_ge(ring_read, ring_total)
            v.memset(r1[:, 0, :], 0.0).then_inc(attn_done, 1)

            l3 = link[0]
            PER3 = 1 + 4 + 5 + 1

            def moments(st, mean_, dev_, step, sync, done):
                d, m2 = dev_[:, 1, :], dev_[:, 2, :]
                step(v.tensor_tensor(mean_, st[:, :, 1], st[:, :, 4], ALU.add))
                step(v.tensor_tensor(d, st[:, :, 1], st[:, :, 4], ALU.subtract))
                step(v.tensor_tensor(m2, st[:, :, 2], st[:, :, 5], ALU.add))
                sync()
                step(v.tensor_scalar(mean_, mean_, 0.5, None, ALU.mult))
                step(v.tensor_tensor(d, d, d, ALU.mult))
                sync()
                v.scalar_tensor_tensor(dev_[:, 0, :], d, D / 4.0, m2, ALU.mult, ALU.add).then_inc(done, 1)

            with ve.Fori(0, NCH // 2) as i:
                at = [0]

                def step3(ins):
                    ins.then_inc(dve, 1)
                    at[0] += 1

                def sync3():
                    ve.wait_ge(dve, i * (2 * PER3) + (l3 + at[0]))

                for k in range(2):
                    n = i * 2 + k
                    ve.wait_ge(wo_done, n + 1)
                    step3(v.tensor_tensor(y1[:, k, :, :], banks[:, 2 + k, :].rearrange("p (t n) -> p t n", t=4),
                                          x_sb[:, bass.ds(n * 4, 4), :], ALU.add))
                    sync3()
                    for t in range(4):
                        step3(v.bn_stats(stats[:, k, t, :], y1[:, k, t, :]))
                    sync3()
                    moments(stats[:, k, :, :], mean[:, k, :], dev[:, k, :, :], step3, sync3, var_done)
                    ve.wait_ge(std_done, n + 1)
                    step3(v.reciprocal(rstd[:, k, :], std[:, k, :]))
                    sync3()
                    for t in range(4):
                        ins = v.tensor_scalar(x1s[:, k, t, :], y1[:, k, t, :], mean[:, k, t:t + 1], rstd[:, k, t:t + 1],
                                              ALU.subtract, ALU.mult)
                    ins.then_inc(x1_done, 1)
                    ve.wait_ge(x1_done, n + 1)
                    v.tensor_copy(attn[:, bass.ds(n * 4, 4), :], x1s[:, k, :, :])
                    ve.wait_ge(lg_done, n + 1)
                    v.tensor_tensor(logits[:, bass.ds(n * 4, 4), :],
                                    banks[:, 6 + k, 0:4 * E].rearrange("p (t e) -> p t e", t=4),
                                    bg_sb[:, :].unsqueeze(1).broadcast_to([P, 4, E]), ALU.add).then_inc(staged2, 1)
            link[0] = l3 + PER3 * NCH

            ve.wait_ge(staged2, NCH)
            bc = lambda a: a.unsqueeze(2).broadcast_to([P, NT, E])
            ib = iota_e[:, :].unsqueeze(1).broadcast_to([P, NT, E])
            chain(v.tensor_reduce(r1[:, 0, :], logits[:, :, :], AX.X, ALU.max))
            v.tensor_tensor(rt[:, 0, :, :], logits[:, :, :], bc(r1[:, 0, :]), ALU.subtract).then_inc(top_in, 1)
            ve.wait_ge(top_exp, 1)
            chain(v.tensor_reduce(r1[:, 1, :], rt[:, 1, :, :], AX.X, ALU.add))
            chain(v.reciprocal(r1[:, 2, :], r1[:, 1, :]))
            chain(v.tensor_tensor(rt[:, 2, :, :], rt[:, 1, :, :], bc(r1[:, 2, :]), ALU.mult))
            ve.wait_ge(iota_done, E + 1)
            left = 2
            for r in range(2):
                src = rt[:, 2 + r, :, :]
                chain(v.tensor_reduce(r1[:, 3, :], src, AX.X, ALU.max))
                chain(v.tensor_tensor(rt[:, 4, :, :], src, bc(r1[:, 3, :]), ALU.is_equal))
                chain(v.tensor_tensor(rt[:, 5, :, :], rt[:, 4, :, :], ib, ALU.mult))
                chain(v.tensor_reduce(r1[:, 4, :], rt[:, 5, :, :], AX.X, ALU.min))
                chain(v.tensor_tensor(rt[:, 6 + r, :, :], ib, bc(r1[:, 4, :]), ALU.is_equal))
                if r == 0:
                    chain(v.scalar_tensor_tensor(rt[:, 3, :, :], rt[:, 6, :, :], -2.0, rt[:, 2, :, :],
                                                 ALU.mult, ALU.add))
            chain(v.tensor_tensor(rt[:, 4, :, :], rt[:, 6, :, :], rt[:, 7, :, :], ALU.add))
            chain(v.tensor_tensor(rt[:, 5, :, :], rt[:, 4, :, :], rt[:, 2, :, :], ALU.mult))
            chain(v.tensor_reduce(r1[:, 5, :], rt[:, 5, :, :], AX.X, ALU.add))
            chain(v.tensor_scalar(r1[:, 6, :], r1[:, 5, :], GATE_EPS, None, ALU.add))
            chain(v.reciprocal(r1[:, 7, :], r1[:, 6, :]))
            chain(v.tensor_tensor(gates[:, :, :], rt[:, 5, :, :], bc(r1[:, 7, :]), ALU.mult))

            l5 = link[0]
            PER5 = E * 4
            with ve.Fori(0, NCH) as n:
                at = [0]

                def step5(ins):
                    ins.then_inc(dve, 1)
                    at[0] += 1

                for e in range(E):
                    ve.wait_ge(y_done, n * E + (e + 1))
                    if e >= 2:
                        ve.wait_ge(dve, n * PER5 + (l5 + at[0] - 4))
                    else:
                        ve.wait_ge(dve, n * PER5 + l5)
                    v.tensor_tensor(yb[:, e % 2, :, :], banks[:, 2 + e % 2, :].rearrange("p (t n) -> p t n", t=4),
                                    b2_sb[:, e, :].unsqueeze(1).broadcast_to([P, 4, D]), ALU.add).then_inc(y_used, 1)
                    ve.wait_ge(y_used, n * E + (e + 1) + 1)
                    ve.wait_ge(dve, n * PER5 + (l5 + at[0]))
                    for t in range(4):
                        x1_t = attn[:, bass.ds(n * 4 + t, 1), :].rearrange("p a b -> p (a b)")
                        step5(v.scalar_tensor_tensor(x1_t, yb[:, e % 2, t, :],
                                                     gates[:, bass.ds(n * 4 + t, 1), e:e + 1].rearrange(
                                                         "p a b -> p (a b)"),
                                                     x1_t, ALU.mult, ALU.add))
                assert at[0] == PER5
            link[0] = l5 + PER5 * NCH

            ve.wait_ge(dve, link[0])

            def step6(ins):
                link[0] += 1
                ins.then_inc(dve, 1)

            for t in range(NT):
                step6(v.bn_stats(stats_all[:, t, :], attn[:, t, :]))
            ve.wait_ge(dve, link[0])
            moments(stats_all[:, :, :], mean_all[:, :], dev_all[:, :, :], step6, lambda: ve.wait_ge(dve, link[0]), var2_done)
            ve.wait_ge(std2_done, 1)
            chain(v.reciprocal(rstd_all[:, :], std_all[:, :]))
            for t in range(NT):
                ins = v.tensor_scalar(x_sb[:, t, :], attn[:, t, :], mean_all[:, t:t + 1], rstd_all[:, t:t + 1],
                                      ALU.subtract, ALU.mult)
                if t % BT == BT - 1:
                    ins.then_inc(fin_ready, 1)

        @block.gpsimd
        def _(pool):
            pp = nc.gpsimd
            pp.memset(fill[:, 0, :], 0.0).then_inc(fill_set, 1)
            pp.memset(fill[:, 1, :], 1.0).then_inc(fill_set, 1)
            pp.memset(eps_sb[:, :], EPS).then_inc(iota_done, 1)
            for e in range(E):
                pp.memset(iota_e[:, e:e + 1], float(e - E)).then_inc(iota_done, 1)
            for c in range(NCH):
                i = c % 2
                pool.wait_ge(part_done, 2 * c + 1)
                pp.tensor_tensor(rem[:, i, 1, :, :], rem[:, i, 0, :, :], parts[:, i, 0, :, :],
                                 ALU.subtract).then_inc(rem_done, 1)
                pool.wait_ge(rem_done, 2 * c + 1)
                pool.wait_ge(part_done, 2 * c + 2)
                pp.tensor_tensor(parts[:, i, 2, :, :], rem[:, i, 1, :, :], parts[:, i, 1, :, :],
                                 ALU.subtract).then_inc(rem_done, 1)
            for i in range(2):
                pool.wait_ge(stored[i], 16 * 12 * (NCH // 2))
            pp.memset(vx[:, :, :, :, :], 0.0).then_inc(vx_set, 1)
            pool.wait_ge(vx_set, 1)
            pp.memset(vx[:, :, :, :, DK:DK + 1], 1.0).then_inc(vx_set, 1)
            pp.memset(zero[:, :, :], 0.0).then_inc(vx_set, 1)
            pool.wait_ge(v_read, NT // 4)

            def v_unit(b, g):
                pool.wait_ge(vx_set, 3)
                pp.tensor_copy(vx[:, g, :, :, 0:DK],
                               v_sb[:, bass.ds(b * BT, BT), g * 32:(g + 1) * 32].rearrange(
                                   "p t (h d) -> p t h d", h=GH)).then_inc(vx_ready, 1)

            def split_max(u, g):
                pool.wait_ge(mx_ready, u + 1)
                neg, r = mx[:, g % 2, :, :], mrem[:, g % 2, :, :]
                part = [msp[:, g % 2, :, j, :] for j in range(3)]
                pp.tensor_tensor(part[0], neg, zero[:, :, :], ALU.add).then_inc(msplit, 1)
                pool.wait_ge(msplit, u * 4 + 1)
                pp.tensor_tensor(r, neg, part[0], ALU.subtract).then_inc(msplit, 1)
                pool.wait_ge(msplit, u * 4 + 2)
                pp.tensor_tensor(part[1], r, zero[:, :, :], ALU.add).then_inc(msplit, 1)
                pool.wait_ge(msplit, u * 4 + 3)
                pp.tensor_tensor(part[2], r, part[1], ALU.subtract).then_inc(msplit, 1)

            v_unit(0, 0)
            split_max(0, 0)

            def batch(b, last):
                for g in range(NG):
                    if last and g == NG - 1:
                        continue
                    nb, ng = b + (g + 1) // NG, (g + 1) % NG
                    if not (isinstance(b, int) and b == 0 and g < 3):
                        if g < 3:
                            pool.wait_ge(pv_done, b * (NG * NB) + 0 + 1) if g == 2 else pool.wait_ge(
                                pv_done, b * (NG * NB) + 1)
                        else:
                            pool.wait_ge(pv_done, b * (NG * NB) + NB + 1)
                    v_unit(nb, ng)
                    split_max(b * NG + g + 1, ng)

            with pool.Fori(0, B - 1) as b:
                batch(b, False)
            batch(B - 1, True)



def kernel(L0_attn_x, L0_attn_W_Q, L0_attn_W_K, L0_attn_W_V, L0_attn_W_O, L0_ffn_Wg, L0_ffn_bg,
           L0_ffn_W1, L0_ffn_b1, L0_ffn_W2, L0_ffn_b2):
    import concourse.bacc as bacc
    from concourse.bass_utils import run_bass_kernel_spmd

    f = lambda a: np.asarray(a)
    x = f(L0_attn_x).reshape(B * S, D)
    flip = np.arange(D).reshape(H, 2, DK // 2)[:, ::-1].reshape(-1)
    WQ, WK = f(L0_attn_W_Q), f(L0_attn_W_K)
    theta = (np.float32(1.0) / np.float32(10000.0) ** (np.arange(0, DK, 2, dtype=np.float32) / np.float32(DK)))
    ang = np.outer(np.arange(S, dtype=np.float32), theta.astype(np.float32)).astype(np.float32)
    ang = np.concatenate([ang, ang], axis=-1)
    sign = np.where(np.arange(DK) < DK // 2, -1.0, 1.0).astype(np.float32)
    cosT = np.tile(np.cos(ang).T, (H, 1)).astype(np.float32)
    sinT = np.tile((np.sin(ang) * sign).T, (H, 1)).astype(np.float32)
    q, k = np.arange(P)[:, None], np.arange(P)[None, :]
    mask_a = np.where(k > q, np.float32(-1e30), np.float32(0.0))
    mask_b = np.where(k < q, np.float32(-1e30), np.float32(0.0))
    arrays = {
        "xT": x.T, "x": x, "wqT": WQ.T, "wqfT": WQ[flip].T, "wkT": WK.T, "wkfT": WK[flip].T,
        "wvT": f(L0_attn_W_V).T, "woT": f(L0_attn_W_O).T, "wg": f(L0_ffn_Wg), "bg": f(L0_ffn_bg),
        "w1": f(L0_ffn_W1), "b1T": f(L0_ffn_b1).reshape(E * HC, P).T, "w2": f(L0_ffn_W2), "b2": f(L0_ffn_b2),
        "cosT": cosT, "sinT": sinT, "ident": np.eye(P, dtype=np.float32),
        "maskA": mask_a, "maskB": mask_b,
    }
    arrays = {n: np.ascontiguousarray(a) for n, a in arrays.items()}
    nc = bacc.Bacc("TRN2", target_bir_lowering=False, num_devices=1)
    args = {n: nc.dram_tensor(f"in_{n}", a.shape, mybir.dt.from_np(a.dtype), kind="ExternalInput").ap()
            for n, a in arrays.items()}
    out = nc.dram_tensor("out_0", (B * S, D), F32, kind="ExternalOutput").ap()
    build(nc, out=out, **args)
    r = run_bass_kernel_spmd(nc, [{f"in_{n}": a for n, a in arrays.items()}], core_ids=[0])
    return r.results[0]["out_0"].reshape(B, S, D)
```

```python
from contextlib import ExitStack

import numpy as np
import concourse.bass as bass
from concourse import mybir

F32 = mybir.dt.float32
BF16 = mybir.dt.bfloat16
ALU = mybir.AluOpType
ACT = mybir.ActivationFunctionType
AX = mybir.AxisListType

P = 128
B, S, D = 4, 1024, 128
H, DK = 16, 8
E, HID = 8, 512
NT = B * S // P
BT = S // P
GH = 4
NG = H // GH
CH = 512
NCH = B * S // CH
HC = HID // P
ROWS = 56
MROW = 32
Q_PLACES = ((0, (0, 3, 6)), (1, (1, 2)), (2, (5,)))
K_PLACES = ((0, (1, 3, 5)), (1, (0, 2)), (2, (6,)))
SCALE = float(np.float32(1.0) / np.sqrt(np.float32(DK)))
EPS = 1e-5
GATE_EPS = 1e-8
TL = 8
NTILE = -(-(2 * B * S // P + E - 1) // TL) * TL
ROW = D + 4
NOWHERE = float(1 << 20)
RING = 3


def pass_a_items():
    items = []
    for sb in range(BT):
        whole, rest = divmod((sb + 1) * P, CH)
        parts = [(CH * i, CH) for i in range(whole)] + ([(CH * whole, rest)] if rest else [])
        for t0, n in parts:
            masked = t0 + n == (sb + 1) * P
            if 2 * n <= CH:
                items += [(par, sb, t0, n, (0, 1), masked) for par in (0, 1)]
            else:
                items += [(par, sb, t0, n, (slot,), masked) for slot in (0, 1) for par in (0, 1)]
    return items


def pass_b_steps():
    steps = []
    for c in range(S // CH):
        for j in range((c + 1) * CH // P):
            s0 = max(P * j, CH * c)
            steps.append((c, j, s0, CH * (c + 1) - s0))
    return steps


A_ITEMS = pass_a_items()
B_STEPS = pass_b_steps()
NA, NB = len(A_ITEMS), len(B_STEPS)
NU = B * NG
C_LAST = [max(k for k, st in enumerate(B_STEPS) if st[0] == c) for c in range(2)]
A_LEAD, A_END = 7, 6


def diagonal(k):
    c, j, s0, n = B_STEPS[k]
    return s0 == P * j


DIAG = [sum(diagonal(i) for i in range(k + 1)) for k in range(NB)]


def a_quota():
    steps = [k % NB for k in range(A_LEAD, NB + A_END + 1)]
    work = [B_STEPS[k][3] for k in steps]
    return [NA * sum(work[:i + 1]) // sum(work) for i in range(len(work))]


def schedule():
    quota = a_quota()
    ev = []
    for v in range(3):
        ev.append(("LOAD", v))
    ev.append(("VX", 0))
    ev += [("A", 0, i) for i in range(NA)] + [("SPLIT", 0)]
    lead = NB - A_LEAD
    ev += [("A", 1, i) for i in range(quota[lead - 1])]
    ev.insert(len(ev) - quota[lead - 1] // 2, ("MT", 0))
    ev.insert(len(ev) - quota[lead - 1] // 2, ("MROWS", 0))
    ev += [("QK", 0), ("QK", 1)]

    def stage3(bt, at):
        return {
            0: [("T1", bt, 0), ("T1", bt, 1)],
            1: [("WO", bt, 0), ("WO", bt, 1)],
            2: [("LNM", bt)],
            3: [("LNA", bt, 0), ("LNA", bt, 1)],
            4: [("T2", bt, 0), ("T2", bt, 1)],
            5: [("LG", bt, 0), ("LG", bt, 1)],
        }[at]

    for u in range(NU):
        for k in range(NB):
            step = u * NB + k
            if k >= A_LEAD:
                v, i = u + 2, k - A_LEAD
            else:
                v, i = u + 1, k + NB - A_LEAD
            items = []
            if v < NU and not (v == 1 and i < lead):
                items = [("A", v, n) for n in range(quota[i - 1] if i else 0, quota[i])]
            half = len(items) // 2
            if k == 3 and u % NG == 1:
                ev.append(("MARK", u))
            if step + 1 < NU * NB:
                ev.append(("QK", 2 * step + 2))
            ev += items[:half]
            if step + 1 < NU * NB:
                ev.append(("QK", 2 * step + 3))
            ev += items[half:]
            if k == A_END and u + 1 < NU:
                ev.append(("SPLIT", u + 1))
            if step:
                ev.append(("PV", step - 1))
                if (step - 1) % NB in C_LAST:
                    ev.append(("EV", 2 * ((step - 1) // NB) + C_LAST.index((step - 1) % NB)))
            for back in (0, 1):
                if step >= 3 and (step - 3) % NB == C_LAST[back]:
                    ev.append(("OT", 2 * ((step - 3) // NB) + back))
            if k == 4 and u + 3 < NU:
                ev.append(("LOAD", u + 3))
            if k == 5 and u + 1 < NU:
                ev.append(("VX", u + 1))
            if k == A_END + 1 and u + 1 < NU:
                ev += [("MT", u + 1), ("MROWS", u + 1)]
            if u % NG == 0 and u > 0 and k in (3, 4, 5, 7, 9, 10):
                ev += stage3(u // NG - 1, (3, 4, 5, 7, 9, 10).index(k))
    last = NU * NB - 1
    ev += [("PV", last), ("EV", 2 * NU - 1), ("OT", 2 * NU - 1)]
    for at in range(6):
        ev += stage3(B - 1, at)
    r, out = 0, []
    for e in ev:
        if e[0] in ("A", "MT", "OT", "T1", "WO", "T2", "LG"):
            out.append((e, r))
            r += 1
        else:
            out.append((e, None))
    return out, r


EVENTS, RING_TOTAL = schedule()
RING_OF = {e: r for e, r in EVENTS if r is not None}
MARKS = [i for i, (e, r) in enumerate(EVENTS) if e[0] == "MARK"]
PROLOGUE, BODY, EPILOGUE = EVENTS[:MARKS[0]], EVENTS[MARKS[0]:MARKS[1]], EVENTS[MARKS[-1]:]
RING_BATCH = sum(r is not None for _, r in BODY)
STRIDE = {"A": NG, "SPLIT": NG, "MT": NG, "MROWS": NG, "LOAD": NG, "VX": NG, "MARK": NG, "QK": 2 * NB * NG,
          "PV": NB * NG, "EV": 2 * NG, "OT": 2 * NG, "T1": 1, "WO": 1, "LNM": 1, "LNA": 1, "T2": 1, "LG": 1}
assert RING_BATCH % RING == 0
for turn in range(1, B - 1):
    moved = [((e[0], e[1] + turn * STRIDE[e[0]]) + e[2:], r if r is None else r + turn * RING_BATCH) for e, r in BODY]
    assert moved == EVENTS[MARKS[turn]:MARKS[turn + 1]]


def first_part(c):
    return max(1, 2 * c)


def second_part(c):
    return 2 * c + 3 if c < NCH - 1 else 2 * NCH


def walk(eng, visit):
    static = lambda n, stride: n
    for e, r in PROLOGUE:
        visit(e, r, static)
    with eng.Fori(0, B - 1) as turn:
        for e, r in BODY:
            visit(e, r, lambda n, stride: turn * stride + n)
    for e, r in EPILOGUE:
        visit(e, r, static)


def build(nc, xT, x, w, wg, bg, w1, b1, w2, b2,
          cs, ident, maskA, before, tile128, tokens, tiles, out):
    ctx = ExitStack()
    with ctx:
        def sb(name, shape, dt=F32):
            return ctx.enter_context(nc.sbuf_tensor(name, shape, dt))

        def sem(name):
            return ctx.enter_context(nc.semaphore(name))

        stack = nc.dram_tensor("stack", [2, B, ROWS // 8, H, 8, S], BF16, kind="Internal").ap()
        pairs = nc.dram_tensor("pairs", [NTILE * P, ROW], F32, kind="Internal").ap()
        results = nc.dram_tensor("results", [2 * B * S, D], F32, kind="Internal").ap()

        xT_sb = sb("xT_sb", [P, B * S])
        x_sb = sb("x_sb", [P, NT, D])
        w_sb = sb("w_sb", [P, 6, D])
        wg_sb = sb("wg_sb", [P, E])
        bg_sb = sb("bg_sb", [P, E])
        w1_sb = sb("w1_sb", [P, E, HID])
        w2_sb = sb("w2_sb", [P, E, HC, D])
        b1_sb = sb("b1_sb", [P, E, HC])
        b2_sb = sb("b2_sb", [P, E, D])
        cs_sb = sb("cs_sb", [P, 2, S])
        id_sb = sb("id_sb", [P, P])
        idb_sb = sb("idb_sb", [P, P], BF16)
        mask_sb = sb("mask_sb", [P, 2, P], BF16)
        mask_f = sb("mask_f", [P, P])
        fill = sb("fill", [P, 2, S], BF16)
        v_sb = sb("v_sb", [P, NT, D])
        attn = sb("attn", [P, BT, D])
        region = sb("region", [P, 16384])
        logits = sb("logits", [P, NT, E])
        rt = xT_sb[:, 0:8 * NT * E].rearrange("p (k t e) -> p k t e", k=8, t=NT)
        r1 = sb("r1", [P, 8, NT])
        iota_e = sb("iota_e", [P, E])
        before_sb = sb("before_sb", [P, 2, P])
        tile128_sb = sb("tile128_sb", [P, NT])
        tokens_sb = sb("tokens_sb", [P, 2, NT])
        tiles_sb = sb("tiles_sb", [P, NTILE])
        cnt = sb("cnt", [P, 2, E, NT])
        small = sb("small", [P, 6, E])
        ends = sb("ends", [P, NTILE, E - 1])
        expert_f = sb("expert_f", [P, NTILE])
        expert = sb("expert", [P, NTILE], mybir.dt.int32)
        slot_f = sb("slot_f", [P, 2, NT])
        slot = sb("slot", [P, 2, NT], mybir.dt.uint32)
        pad = sb("pad", [P, ROW])
        dest = sb("dest", [P, TL, 1], mybir.dt.uint32)

        flat = lambda a: a.rearrange("p a n -> p (a n)")
        rot = flat(w1_sb[:, :, :]).rearrange("p (b t w n) -> p b t w n", b=2, t=2, w=2)
        rem = w2_sb[:, :, :, :].rearrange("p e c n -> p (e c n)").rearrange(
            "p (b t w n) -> p b t w n", b=2, t=2, w=2)
        parts = flat(x_sb[:, :, :])[:, 0:3072].bitcast(BF16).rearrange("p (b j w n) -> p b j w n", b=2, j=3, w=2)
        qst = region[:, 0:4096].bitcast(BF16).rearrange("p (g s n) -> p g s n", g=NG, s=2)
        kst = region[:, 4096:8192].bitcast(BF16).rearrange("p (g s n) -> p g s n", g=NG, s=2)
        probs = [a[:, i, :, :] for a, n in ((region[:, 8192:12288], 4),
                                            (cs_sb[:, :, :].rearrange("p a n -> p (a n)"), 2))
                 for a in (a.rearrange("p (k w n) -> p k w n", k=n, w=2),) for i in range(n)]
        vx = region[:, 12288:16384].rearrange("p (g t h c) -> p g t h c", g=NG, t=BT, h=GH)
        ot = sb("ot", [P, 2, CH])
        rden = sb("rden", [P, 2, 4 * GH])
        mx = sb("mx", [P, 2, GH, BT])
        mx2 = sb("mx2", [P, 2, GH, BT // 2])
        mrem = sb("mrem", [P, 2, GH, BT])
        zero = sb("zero", [P, GH, BT])
        msp = sb("msp", [P, 2, 2, 3, 2, BT], BF16)
        mparts = sb("mparts", [GH * 3 * BT, 2, P], BF16)
        aT = sb("aT", [P, 2, CH])
        y1 = sb("y1", [P, 2, 4, D])
        x1s = sb("x1s", [P, 2, 4, D])
        nwt = sb("nwt", [P, 2, BT])
        xr = region[:, 5120:5120 + 2 * NT * ROW].rearrange("p (t k n) -> p t k n", t=NT, k=2)
        xg = region[:, 13568:13568 + TL * ROW].rearrange("p (b n) -> p b n", b=TL)
        xgT = region[:, 0:256].rearrange("p (b n) -> p b n", b=2)
        hb = region[:, 256:1280].rearrange("p (b n) -> p b n", b=2)
        hg = region[:, 1280:2304].rearrange("p (b n) -> p b n", b=2)
        w1e = region[:, 2304:3328].rearrange("p (b n) -> p b n", b=2)
        yb = region[:, 3328:3584].rearrange("p (b n) -> p b n", b=2)
        ys = region[:, 3584:4608].rearrange("p (b n) -> p b n", b=TL)
        back = [a.rearrange("p (k t n) -> p k t n", k=2, n=D) for a in (xT_sb[:, :], region[:, 0:4096])]
        stats = sb("stats", [P, BT, 6])
        mean = sb("mean", [P, BT])
        dev = sb("dev", [P, 3, BT])
        rstd = sb("rstd", [P, BT])
        stats_all = sb("stats_all", [P, NT, 6])
        mean_all = sb("mean_all", [P, NT])
        dev_all = sb("dev_all", [P, 3, NT])
        rstd_all = sb("rstd_all", [P, NT])

        banks = ctx.enter_context(nc.psum_tensor("banks", [P, 8, CH], F32))
        ring = banks[:, 0:RING, :]
        score = banks[:, RING:RING + 4, :].rearrange("p (k w) n -> p k w n", k=2)
        pv = banks[:, RING + 4, :]

        weights_in = sem("weights_in")
        xT_in = [sem(f"xT_in{b}") for b in range(B)]
        loads = sem("loads")
        x_in = sem("x_in")
        late_in = sem("late_in")
        fill_set = sem("fill_set")
        masks_ready = sem("masks_ready")
        fills = sem("fills")
        proj_done = sem("proj_done")
        proj_read = sem("proj_read")
        rotated = sem("rotated")
        part_done = sem("part_done")
        rem_done = sem("rem_done")
        last_done = sem("last_done")
        stored = [[sem(f"stored{i}_{part}") for part in range(3)] for i in range(2)]
        v_done = sem("v_done")
        v_read = sem("v_read")
        vx_set = sem("vx_set")
        dma_unit = [sem(f"unit_loaded{g}") for g in range(NG)]
        vx_ready = sem("vx_ready")
        ring_full = sem("ring_full")
        ring_read = sem("ring_read")
        mx_ready = sem("mx_ready")
        msplit = sem("msplit")
        mrows = [sem(f"mrows{i}") for i in range(2)]
        qk_done = sem("qk_done")
        exp_done = sem("exp_done")
        pv_done = sem("pv_done")
        ot_ready = sem("ot_ready")
        rden_ready = sem("rden_ready")
        masked = sem("masked")
        mask_turns = sem("mask_turns")
        dve = sem("dve")
        ln = sem("ln")
        x1_done = sem("x1_done")
        iota_done = sem("iota_done")
        top_in = sem("top_in")
        top_mask = sem("top_mask")
        top_exp = sem("top_exp")
        gates_done = sem("gates_done")
        turns_out = sem("turns_out")
        padded = sem("padded")
        counted = sem("counted")
        slots_ready = sem("slots_ready")
        pairs_out = sem("pairs_out")
        pair_in = [sem(f"pair_in{k}") for k in range(TL)]
        xg_turned = sem("xg_turned")
        xgT_ready = sem("xgT_ready")
        h_done = sem("h_done")
        hb_ready = sem("hb_ready")
        gelu_done = sem("gelu_done")
        w1e_ready = sem("w1e_ready")
        y_done = sem("y_done")
        y_read = sem("y_read")
        ys_ready = sem("ys_ready")
        result_out = [sem(f"result_out{k}") for k in range(TL)]
        back_in = [sem(f"back_in{k}") for k in range(2)]
        fin_ready = sem("fin_ready")
        out_done = sem("out_done")

        N_LOADS = 10
        block = ctx.enter_context(nc.Block())

        @block.sync
        def _(sp):
            sp.dma_start(w_sb[:, :, :], w).then_inc(weights_in, 16)
            for b in range(B):
                sp.dma_start(xT_sb[:, b * S:(b + 1) * S], xT[:, b * S:(b + 1) * S]).then_inc(xT_in[b], 16)
                if b == 0:
                    sp.dma_start(cs_sb[:, :, :], cs).then_inc(weights_in, 16)
                    sp.wait_ge(fill_set, 2)
                    for w_ in range(2):
                        sp.dma_start(stack[w_, :, MROW // 8].rearrange("b h r n -> (h r) b n"),
                                     fill[:, w_:w_ + 1, :].broadcast_to([P, B, S])).then_inc(fills, 16)
            sp.dma_start(id_sb[:, :], ident).then_inc(loads, 16)
            sp.dma_start(mask_f[:, :], maskA).then_inc(loads, 16)
            sp.dma_start(wg_sb[:, :], wg).then_inc(loads, 16)
            sp.dma_start(bg_sb[:, :], bg.partition_broadcast(P)).then_inc(loads, 16)
            sp.dma_start(before_sb[:, :, :], before).then_inc(loads, 16)
            sp.dma_start(tile128_sb[:, :], tile128).then_inc(loads, 16)
            sp.dma_start(tokens_sb[:, :, :], tokens).then_inc(loads, 16)
            sp.dma_start(tiles_sb[:, :], tiles).then_inc(loads, 16)
            sp.dma_start(b1_sb[:, :, :], b1).then_inc(loads, 16)
            sp.dma_start(b2_sb[:, :, :], b2.partition_broadcast(P)).then_inc(loads, 16)

            def store(c, part):
                b, i = divmod(c, 2)
                for w_, places in ((0, Q_PLACES), (1, K_PLACES)):
                    blocks = places[part][1]
                    step = blocks[1] - blocks[0] if len(blocks) > 1 else 1
                    sp.dma_start(stack[w_, b, blocks[0]:blocks[-1] + 1:step, :, :, i * CH:(i + 1) * CH]
                                 .rearrange("z h r n -> (h r) z n"),
                                 parts[:, i, part, w_, :].unsqueeze(1).broadcast_to([P, len(blocks), CH])
                                 ).then_inc(stored[i][part], 16)

            def load_unit(b, g):
                for w_, dst in ((0, qst), (1, kst)):
                    for par in (0, 1):
                        for slot_ in (0, 1):
                            src = stack[w_, bass.ds(b, 1), :, GH * g + 2 * slot_ + par, :, :]
                            sp.dma_start(dst[64 * par:64 * par + ROWS, g, slot_, :],
                                         src.rearrange("o z r n -> (o z) r n")).then_inc(dma_unit[g], 16)

            for c in range(NCH + 1):
                if c < NCH:
                    sp.wait_ge(part_done, first_part(c))
                    store(c, 0)
                if c >= 1:
                    sp.wait_ge(part_done, second_part(c - 1))
                    store(c - 1, 1)
                    sp.wait_ge(last_done, c)
                    store(c - 1, 2)
                if c == 3:
                    sp.wait_ge(fills, 16 * 2)
                    for i in range(2):
                        for part in range(3):
                            sp.wait_ge(stored[i][part], 16 * 2)
                    load_unit(0, 0)
            load_unit(0, 1)
            load_unit(0, 2)

            def visit(e, r, at):
                if e[0] == "LOAD":
                    v = e[1]
                    if v >= NG:
                        sp.wait_ge(qk_done, at(2 * NB * (v - 3), 2 * NB * NG))
                    if v >= 3:
                        load_unit(at(v // NG, 1), v % NG)
                    if v == 3:
                        sp.wait_ge(last_done, NCH)
                        sp.dma_start(w1_sb[:, :, :], w1.rearrange("e p n -> p e n")).then_inc(late_in, 16)
                        sp.dma_start(w2_sb[:, :, :, :], w2.rearrange("e (c p) n -> p e c n", p=P)
                                     ).then_inc(late_in, 16)
                elif e[0] == "MROWS":
                    v = e[1]
                    sp.wait_ge(ring_read, at(RING_OF[("MT", v)] + 1, RING_BATCH))
                    for par in (0, 1):
                        sp.dma_start(qst[64 * par + MROW:64 * par + MROW + 3, v % NG, :, :],
                                     mparts[par * 6 * BT:(par + 1) * 6 * BT, v % 2, :]).then_inc(mrows[v % 2], 16)
                    if v == 0:
                        for i in range(2):
                            for part in range(3):
                                sp.wait_ge(stored[i][part], 16 * 2 * (NCH // 2))
                        sp.dma_start(x_sb[:, :, :], x.rearrange("(t p) n -> p t n", p=P)).then_inc(x_in, 16)
                    elif v == 1:
                        sp.wait_ge(iota_done, 3)
                        sp.dma_start(pairs.rearrange("(t p) n -> p t n", p=P), pad[:, :].unsqueeze(1).broadcast_to(
                            [P, NTILE, ROW])).then_inc(padded, 16)

            walk(sp, visit)

            for k in range(2):
                sp.wait_ge(pairs_out, 16 * 2 * NT)
            for k in range(TL):
                sp.dma_start(xg[:, k, :], pairs[k * P:(k + 1) * P, :]).then_inc(pair_in[k], 16)
            with sp.Fori(1, NTILE // TL) as i:
                for k in range(TL):
                    sp.wait_ge(ys_ready, i * TL + (k + 1 - TL))
                    sp.dma_start(xg[:, k, :], pairs.rearrange("(t p) n -> t p n", p=P)[bass.ds(i * TL + k, 1)]
                                 .rearrange("o p n -> p (o n)")).then_inc(pair_in[k], 16)
            for k in range(TL):
                sp.wait_ge(result_out[k], 16 * (NTILE // TL))
            half = B * S // 2
            for b in range(2):
                for k in range(2):
                    sp.dma_start(back[b][:, k, :, :], results[k * B * S + b * half:k * B * S + (b + 1) * half, :]
                                 .rearrange("(t p) n -> p t n", p=P)).then_inc(back_in[b], 16)
            for b in range(B):
                sp.wait_ge(fin_ready, b + 1)
                sp.dma_start(out.rearrange("(b t p) n -> b p t n", b=B, p=P)[b], x_sb[:, b * BT:(b + 1) * BT, :]
                             ).then_inc(out_done, 16)
            sp.wait_ge(out_done, 16 * B)

        @block.tensor
        def _(pe):
            mm = nc.tensor.matmul
            pe.wait_ge(weights_in, 32)
            for c in range(NCH):
                bank = 4 * (c % 2)
                if c % 2 == 0:
                    pe.wait_ge(xT_in[c // 2], 16)
                if c >= 2:
                    pe.wait_ge(proj_read, c - 1)
                for i, w in enumerate((0, 2, 1, 3)):
                    last = mm(banks[:, bank + i, :], w_sb[:, w, :], xT_sb[:, c * CH:(c + 1) * CH],
                              start=True, stop=True)
                last.then_inc(proj_done, 1)
            for c in range(NT // 4):
                pe.wait_ge(proj_read, NCH - 1 if c < 4 else NCH)
                for t in range(4):
                    tile = 4 * c + t
                    last = mm(banks[:, c, t * P:(t + 1) * P], xT_sb[:, tile * P:(tile + 1) * P],
                              w_sb[:, 4, :], start=(t == 0), stop=True, skip_group_check=True)
                last.then_inc(v_done, 1)

            pe.wait_ge(masks_ready, 2)
            pe.wait_ge(v_read, RING)

            def visit(e, r, at):
                kind = e[0]
                if r is not None and r >= RING:
                    pe.wait_ge(ring_read, at(r - RING + 1, RING_BATCH))
                bank = None if r is None else r % RING
                if kind == "A":
                    v, i = e[1:]
                    if i == 0:
                        pe.wait_ge(dma_unit[v % NG], at(128 * (v // NG + 1), 128))
                    par, sb_, t0, n, slots, is_masked = A_ITEMS[i]
                    rows = slice(64 * par, 64 * par + ROWS)
                    for m, slot_ in enumerate(slots):
                        last = mm(ring[:, bank, m * n:(m + 1) * n], qst[rows, v % NG, slot_, sb_ * P:(sb_ + 1) * P],
                                  kst[rows, v % NG, slot_, t0:t0 + n], start=(m == 0), stop=not is_masked,
                                  skip_group_check=True)
                    if is_masked:
                        k = len(slots)
                        view = ring[:, bank, 0:k * n].rearrange("p (k n) -> p k n", k=k)[:, :, n - P:n]
                        last = mm(view, idb_sb[:, :], mask_sb[:, 0:k, :], start=False, stop=True,
                                  skip_group_check=True)
                    last.then_inc(ring_full, 1)
                elif kind == "MT":
                    v = e[1]
                    pe.wait_ge(msplit, at(4 * (v + 1), 4 * NG))
                    nc.tensor.transpose(ring[0:GH * 3 * BT, bank, 0:P // 2].bitcast(BF16),
                                        msp[:, v % 2, :, :, :, :].rearrange("p a j s n -> p (a j s n)"),
                                        idb_sb[:, :]).then_inc(ring_full, 1)
                elif kind == "QK":
                    i = e[1]
                    u, k = divmod(i // 2, NB)
                    c, j, s0, n = B_STEPS[k]
                    slot_ = i % 2
                    if i == 0:
                        pe.wait_ge(v_read, NT // 4)
                    if k == 0 and slot_ == 0:
                        pe.wait_ge(mrows[u % 2], at(32 * (u // 2 + 1), 32 * NG // 2))
                    if i >= 2:
                        pe.wait_ge(exp_done, at(i - 1, 2 * NB * NG))
                    for par in (0, 1):
                        rows = slice(64 * par, 64 * par + ROWS)
                        last = mm(score[:, slot_, par, 0:n], kst[rows, u % NG, slot_, j * P:(j + 1) * P],
                                  qst[rows, u % NG, slot_, s0:s0 + n], start=True, stop=True)
                    last.then_inc(qk_done, 1)
                elif kind == "PV":
                    u, k = divmod(e[1], NB)
                    c, j, s0, n = B_STEPS[k]
                    if k == 0:
                        pe.wait_ge(vx_ready, at(u + 1, NG))
                    if j == 0 and 2 * u + c > 0:
                        pe.wait_ge(ot_ready, at(2 * u + c, 2 * NG))
                    if diagonal(k):
                        pe.wait_ge(masked, at(2 * (u * DIAG[-1] + DIAG[k]), 2 * NG * DIAG[-1]))
                    else:
                        pe.wait_ge(exp_done, at(2 * e[1] + 2, 2 * NB * NG))
                    for slot_ in (0, 1):
                        for par in (0, 1):
                            h = 2 * slot_ + par
                            last = mm(pv[32 * h:32 * h + 32, s0 - c * CH:s0 - c * CH + n],
                                      vx[:, u % NG, j, h, :], probs[(2 * e[1] + slot_) % 6][:, par, 0:n],
                                      start=(j == 0), stop=(k == C_LAST[c]),
                                      tile_position=(0, 32 * h), skip_group_check=True)
                    last.then_inc(pv_done, 1)
                elif kind == "OT":
                    n = e[1]
                    pe.wait_ge(ot_ready, at(n + 1, 2 * NG))
                    for t in range(4):
                        last = nc.tensor.transpose(ring[:, bank, t * P:(t + 1) * P],
                                                   ot[:, n % 2, t * P:(t + 1) * P], id_sb[:, :])
                    last.then_inc(ring_full, 1)
                elif kind in ("T1", "WO", "T2", "LG"):
                    bt, c = e[1:]
                    if kind == "T1":
                        pe.wait_ge(ring_read, at(RING_OF[("OT", 2 * NG * bt + 2 * NG - 1)] + 1, RING_BATCH))
                    elif kind == "WO":
                        pe.wait_ge(ring_read, at(RING_OF[("T1", bt, c)] + 1, RING_BATCH))
                    elif kind == "T2":
                        pe.wait_ge(x1_done, at(2 * bt + c + 1, 2))
                    else:
                        pe.wait_ge(ring_read, at(RING_OF[("T2", bt, c)] + 1, RING_BATCH))
                    for t in range(4):
                        cols = slice(t * P, (t + 1) * P)
                        if kind == "T1":
                            last = nc.tensor.transpose(ring[:, bank, cols], attn[:, 4 * c + t, :], id_sb[:, :])
                        elif kind == "WO":
                            last = mm(ring[:, bank, cols], aT[:, c, cols], w_sb[:, 5, :], start=(t == 0), stop=True,
                                      skip_group_check=True)
                        elif kind == "T2":
                            last = nc.tensor.transpose(ring[:, bank, cols], x1s[:, c, t, :], id_sb[:, :])
                        else:
                            last = mm(ring[:, bank, t * E:(t + 1) * E], aT[:, c, cols], wg_sb[:, :],
                                      start=(t == 0), stop=True, skip_group_check=True)
                    last.then_inc(ring_full, 1)

            walk(pe, visit)
            pe.wait_ge(ring_read, RING_TOTAL)

            pe.wait_ge(top_mask, 1)
            for k in range(2):
                last = mm(banks[:, k, 0:NT * E], before_sb[:, k, :], rt[:, 4, :, :], start=True, stop=True)
            last.then_inc(counted, 1)

            pe.wait_ge(slots_ready, 1)
            pe.wait_ge(late_in, 32)

            def stage_down(turn, k):
                e = pe.value_load(expert[0:1, bass.ds(turn * TL + k, 1)], min_val=0, max_val=E - 1)
                pe.wait_ge(gelu_done, turn * TL + (k + 1))
                if not first_use(turn, k):
                    pe.wait_ge(y_read, turn * TL + (k - 1))
                for hc in range(HC):
                    last = mm(banks[:, 6 + k % 2, 0:D], hg[:, k % 2, hc * P:(hc + 1) * P],
                              w2_sb[:, bass.ds(e, 1), hc, :].rearrange("p a n -> p (a n)"),
                              start=(hc == 0), stop=(hc == HC - 1))
                last.then_inc(y_done, 1)

            def stage_up(turn, k):
                pe.wait_ge(w1e_ready, turn * TL + (k + 1))
                pe.wait_ge(xgT_ready, turn * TL + (k + 1))
                if not first_use(turn, k):
                    pe.wait_ge(hb_ready, turn * TL + (k - 1))
                for hc in range(HC):
                    last = mm(banks[:, 2 + k % 2, hc * P:(hc + 1) * P], w1e[:, k % 2, hc * P:(hc + 1) * P],
                              xgT[:, k % 2, :], start=(hc == 0), stop=(hc == HC - 1), skip_group_check=True)
                last.then_inc(h_done, 1)

            def stage_tx(turn, k):
                pe.wait_ge(pair_in[k], turn * 16 + 16)
                if not first_use(turn, k):
                    pe.wait_ge(xgT_ready, turn * TL + (k - 1))
                nc.tensor.transpose(banks[:, k % 2, 0:P], xg[:, k, 0:D], id_sb[:, :]).then_inc(xg_turned, 1)

            pipeline(pe, ((stage_down, 0), (stage_up, 2), (stage_tx, 3)))

        @block.scalar
        def _(act):
            for c in range(NCH + 1):
                if c < NCH:
                    i = c % 2
                    act.wait_ge(rotated, c + 1)
                    if c >= 2:
                        act.wait_ge(stored[i][0], 16 * 2 * (c // 2))
                    nc.scalar.copy(parts[:, i, 0, :, :], rem[:, i, 0, :, :]).then_inc(part_done, 1)
                if c == NCH:
                    for k in range(NT // 4):
                        act.wait_ge(v_done, k + 1)
                        nc.scalar.copy(v_sb[:, 4 * k:4 * k + 4, :],
                                       banks[:, k, :].rearrange("p (t n) -> p t n", t=4)).then_inc(v_read, 1)
                if c >= 1:
                    i = (c - 1) % 2
                    act.wait_ge(rem_done, c)
                    if c >= 3:
                        act.wait_ge(stored[i][1], 16 * 2 * ((c - 1) // 2))
                    nc.scalar.copy(parts[:, i, 1, :, :], rem[:, i, 1, :, :]).then_inc(part_done, 1)
            def visit(e, r, at):
                if e[0] == "QK":
                    i = e[1]
                    n = B_STEPS[i // 2 % NB][3]
                    act.wait_ge(qk_done, at(i + 1, 2 * NB * NG))
                    if i // 2 >= 3:
                        act.wait_ge(pv_done, at(i // 2 - 2, NB * NG))
                    nc.scalar.activation(probs[i % 6][:, :, 0:n], score[:, i % 2, :, 0:n], ACT.Exp,
                                         scale=SCALE).then_inc(exp_done, 1)
                elif e[0] == "EV":
                    n = e[1]
                    act.wait_ge(pv_done, at(n // 2 * NB + C_LAST[n % 2] + 1, NB * NG))
                    if n >= 2:
                        act.wait_ge(ring_full, at(RING_OF[("OT", n - 2)] + 1, RING_BATCH))
                    nc.scalar.copy(ot[:, n % 2, :], pv[:, :]).then_inc(ot_ready, 1)

            walk(act, visit)

            act.wait_ge(top_in, 1)
            nc.scalar.activation(rt[:, 1, :, :], rt[:, 0, :, :], ACT.Exp).then_inc(top_exp, 1)

            def stage_tx(turn, k):
                act.wait_ge(xg_turned, turn * TL + (k + 1))
                if not first_use(turn, k):
                    act.wait_ge(h_done, turn * TL + (k - 1))
                nc.scalar.copy(xgT[:, k % 2, :], banks[:, k % 2, 0:P]).then_inc(xgT_ready, 1)

            def stage_gelu(turn, k):
                act.wait_ge(hb_ready, turn * TL + (k + 1))
                if not first_use(turn, k):
                    act.wait_ge(y_done, turn * TL + (k - 1))
                nc.scalar.activation(hg[:, k % 2, :], hb[:, k % 2, :], ACT.Gelu_apprx_tanh).then_inc(gelu_done, 1)

            def stage_w1(turn, k):
                e = act.value_load(expert[0:1, bass.ds(turn * TL + k, 1)], min_val=0, max_val=E - 1)
                if not first_use(turn, k):
                    act.wait_ge(h_done, turn * TL + (k - 1))
                nc.scalar.copy(w1e[:, k % 2, :], w1_sb[:, bass.ds(e, 1), :].rearrange("p a n -> p (a n)")
                               ).then_inc(w1e_ready, 1)

            act.wait_ge(slots_ready, 1)
            act.wait_ge(late_in, 32)
            pipeline(act, ((stage_tx, 2), (stage_gelu, 1), (stage_w1, 3)))

        @block.vector
        def _(ve):
            v = nc.vector
            link = [0]

            def chain(ins):
                link[0] += 1
                ins.then_inc(dve, 1)
                ve.wait_ge(dve, link[0])

            ve.wait_ge(weights_in, 32)
            for c in range(NCH):
                i = c % 2
                h = c % 2
                bank = 4 * i
                ve.wait_ge(proj_done, c + 1)
                if c >= 2:
                    ve.wait_ge(rem_done, c - 1)
                cos = cs_sb[:, 0, h * CH:(h + 1) * CH].unsqueeze(1).broadcast_to([P, 2, CH])
                sin = cs_sb[:, 1, h * CH:(h + 1) * CH].unsqueeze(1).broadcast_to([P, 2, CH])
                v.tensor_tensor(rot[:, i, 0, :, :], banks[:, bank:bank + 2, :], cos, ALU.mult).then_inc(dve, 1)
                link[0] += 1
                v.tensor_tensor(rot[:, i, 1, :, :], banks[:, bank + 2:bank + 4, :], sin,
                                ALU.mult).then_inc(proj_read, 1)
                ve.wait_ge(dve, link[0])
                ve.wait_ge(proj_read, c + 1)
                v.tensor_tensor(rem[:, i, 0, :, :], rot[:, i, 0, :, :], rot[:, i, 1, :, :],
                                ALU.add).then_inc(rotated, 1)
            ve.wait_ge(loads, 16 * N_LOADS)
            v.tensor_copy(idb_sb[:, :], id_sb[:, :]).then_inc(masks_ready, 1)
            v.tensor_copy(mask_sb[:, :, :], mask_f[:, :].unsqueeze(1).broadcast_to([P, 2, P])
                          ).then_inc(masks_ready, 1)
            def moments(st, mean_, dev_, step, sync):
                d, m2 = dev_[:, 1, :], dev_[:, 2, :]
                step(v.tensor_tensor(mean_, st[:, :, 1], st[:, :, 4], ALU.add))
                step(v.tensor_tensor(d, st[:, :, 1], st[:, :, 4], ALU.subtract))
                step(v.tensor_tensor(m2, st[:, :, 2], st[:, :, 5], ALU.add))
                sync()
                step(v.tensor_scalar(mean_, mean_, 0.5, None, ALU.mult))
                step(v.tensor_tensor(d, d, d, ALU.mult))
                sync()
                step(v.scalar_tensor_tensor(dev_[:, 0, :], d, D / 4.0, m2, ALU.mult, ALU.add))
                sync()

            def inverse_root(y, var, t, step, sync):
                i32 = mybir.dt.int32
                step(v.tensor_scalar(y.bitcast(i32), var.bitcast(i32), 1, None, ALU.arith_shift_right))
                sync()
                step(v.tensor_scalar(y.bitcast(i32), y.bitcast(i32), -1.0, float(0x5f3759df), ALU.mult, ALU.add))
                for _ in range(3):
                    sync()
                    step(v.tensor_tensor(t, y, y, ALU.mult))
                    sync()
                    step(v.scalar_tensor_tensor(t, t, -0.5, var, ALU.mult, ALU.mult))
                    sync()
                    step(v.scalar_tensor_tensor(y, t, 1.5, y, ALU.add, ALU.mult))
                sync()

            PER_LN = 2 + 8 + 6 + 1 + 2 + 9

            def visit(e, r, at):
                kind = e[0]
                if r is not None:
                    bank = r % RING
                    ve.wait_ge(ring_full, at(r + 1, RING_BATCH))

                def read(ins):
                    ins.then_inc(ring_read, 1)

                if kind == "A":
                    unit, i = e[1:]
                    par, sb_, t0, n, slots, is_masked = A_ITEMS[i]
                    hs = slice(2 * slots[0] + par, 2 * slots[-1] + par + 1, 2)
                    dst = mx[:, unit % 2, hs, sb_] if t0 == 0 else mx2[:, unit % 2, hs, sb_ - BT // 2]
                    src = ring[:, bank, 0:len(slots) * n].rearrange("p (k n) -> p k n", k=len(slots))
                    read(v.tensor_reduce(dst, src, AX.X, ALU.max, negate=True))
                    if i == NA - 1:
                        ve.wait_ge(ring_read, at(r + 1, RING_BATCH))
                        v.tensor_tensor(mx[:, unit % 2, :, BT // 2:BT], mx[:, unit % 2, :, BT // 2:BT],
                                        mx2[:, unit % 2, :, :], ALU.min).then_inc(mx_ready, 1)
                elif kind == "MT":
                    read(v.tensor_copy(mparts[:, e[1] % 2, :], ring[0:GH * 3 * BT, bank, 0:P // 2].bitcast(BF16)))
                elif kind == "OT":
                    n = e[1]
                    g, c = n // 2 % NG, n % 2
                    view = ring[:, bank, :].rearrange("p (t h d) -> p t h d", t=4, h=GH)
                    inv = rden[:, c, :].rearrange("p (t h) -> p t h", t=4)
                    v.reciprocal(inv, view[:, :, :, DK]).then_inc(rden_ready, 1)
                    ve.wait_ge(rden_ready, at(n + 1, 2 * NG))
                    read(v.tensor_tensor(attn[:, c * 4:c * 4 + 4, g * 32:(g + 1) * 32].rearrange(
                                             "p t (h d) -> p t h d", h=GH),
                                         view[:, :, :, 0:DK], inv.unsqueeze(3).broadcast_to([P, 4, GH, DK]),
                                         ALU.mult))
                elif kind in ("T1", "T2"):
                    read(v.tensor_copy(aT[:, e[2], :], ring[:, bank, :]))
                elif kind == "LG":
                    bt, c = e[1:]
                    read(v.tensor_tensor(logits[:, bass.ds(at(bt * BT + 4 * c, BT), 4), :],
                                         ring[:, bank, 0:4 * E].rearrange("p (t e) -> p t e", t=4),
                                         bg_sb[:, :].unsqueeze(1).broadcast_to([P, 4, E]), ALU.add))
                elif kind == "WO":
                    bt, c = e[1:]
                    ve.wait_ge(x_in, 16)
                    read(v.tensor_tensor(y1[:, c, :, :], ring[:, bank, :].rearrange("p (t n) -> p t n", t=4),
                                         x_sb[:, bass.ds(at(bt * BT + 4 * c, BT), 4), :], ALU.add))
                elif kind == "LNM":
                    bt = e[1]
                    done = [bt * PER_LN]

                    def step(ins):
                        ins.then_inc(ln, 1)
                        done[0] += 1

                    sync = lambda: ve.wait_ge(ln, at(done[0], PER_LN))
                    ve.wait_ge(ring_read, at(RING_OF[("WO", bt, 1)] + 1, RING_BATCH))
                    for t in range(BT):
                        step(v.bn_stats(stats[:, t, :], y1[:, t // 4, t % 4, :]))
                    sync()
                    moments(stats[:, :, :], mean[:, :], dev[:, :, :], step, sync)
                    step(v.tensor_scalar(dev[:, 1, :], dev[:, 0, :], 1.0 / D, EPS, ALU.mult, ALU.add))
                    sync()
                    inverse_root(rstd[:, :], dev[:, 1, :], nwt[:, 0, :], step, sync)
                    assert done[0] == bt * PER_LN + 8 + 6 + 1 + 2 + 9
                    for c in range(2):
                        step(v.tensor_copy(nwt[:, 1, c:c + 1], rstd[:, c:c + 1]))
                    assert done[0] == (bt + 1) * PER_LN
                elif kind == "LNA":
                    bt, c = e[1:]
                    for t in range(4):
                        k = 4 * c + t
                        v.tensor_scalar(x_sb[:, bass.ds(at(bt * BT + k, BT), 1), :].rearrange("p a n -> p (a n)"),
                                        y1[:, c, t, :], mean[:, k:k + 1], rstd[:, k:k + 1],
                                        ALU.subtract, ALU.mult)
                        last = v.tensor_scalar(x1s[:, c, t, :], y1[:, c, t, :], mean[:, k:k + 1],
                                               rstd[:, k:k + 1], ALU.subtract, ALU.mult)
                    last.then_inc(x1_done, 1)

            walk(ve, visit)
            ve.wait_ge(pv_done, NU * NB)
            ve.wait_ge(ring_read, RING_TOTAL)
            for w in range(2):
                v.tensor_copy(xr[:, :, w, 0:D], x_sb[:, :, :])

            bc = lambda a: a.unsqueeze(2).broadcast_to([P, NT, E])
            ib = iota_e[:, :].unsqueeze(1).broadcast_to([P, NT, E])
            chain(v.tensor_reduce(r1[:, 0, :], logits[:, :, :], AX.X, ALU.max))
            v.tensor_tensor(rt[:, 0, :, :], logits[:, :, :], bc(r1[:, 0, :]), ALU.subtract).then_inc(top_in, 1)
            ve.wait_ge(top_exp, 1)
            chain(v.tensor_reduce(r1[:, 1, :], rt[:, 1, :, :], AX.X, ALU.add))
            chain(v.reciprocal(r1[:, 2, :], r1[:, 1, :]))
            chain(v.tensor_tensor(rt[:, 2, :, :], rt[:, 1, :, :], bc(r1[:, 2, :]), ALU.mult))
            ve.wait_ge(iota_done, E + 3)
            left = 2
            for r in range(2):
                src = rt[:, 2 + r, :, :]
                top = r1[:, 3 + 3 * r, :]
                chain(v.tensor_reduce(top, src, AX.X, ALU.max))
                chain(v.tensor_tensor(rt[:, 4, :, :], src, bc(top), ALU.is_equal))
                chain(v.tensor_tensor(rt[:, 5, :, :], rt[:, 4, :, :], ib, ALU.mult))
                chain(v.tensor_reduce(r1[:, 4, :], rt[:, 5, :, :], AX.X, ALU.min))
                chain(v.tensor_tensor(rt[:, 6 + r, :, :], ib, bc(r1[:, 4, :]), ALU.is_equal))
                if r == 0:
                    chain(v.scalar_tensor_tensor(rt[:, 3, :, :], rt[:, 6, :, :], -2.0, rt[:, 2, :, :],
                                                 ALU.mult, ALU.add))
            v.tensor_tensor(rt[:, 4, :, :], rt[:, 6, :, :], rt[:, 7, :, :], ALU.add).then_inc(top_mask, 1)
            chain(v.tensor_tensor(r1[:, 5, :], r1[:, 3, :], r1[:, 6, :], ALU.add))
            chain(v.tensor_scalar(r1[:, 5, :], r1[:, 5, :], GATE_EPS, None, ALU.add))
            chain(v.reciprocal(r1[:, 7, :], r1[:, 5, :]))
            chain(v.tensor_tensor(xr[:, :, 0, D], r1[:, 3, :], r1[:, 7, :], ALU.mult))
            chain(v.tensor_tensor(xr[:, :, 1, D], r1[:, 6, :], r1[:, 7, :], ALU.mult))
            for w in range(2):
                chain(v.tensor_copy(xr[:, :, w, D + 1], tokens_sb[:, w, :]))
            chain(v.memset(xr[:, :, :, D + 2:ROW], 0.0))
            ve.wait_ge(counted, 1)
            chain(v.tensor_copy(cnt[:, 0, :, :], banks[:, 1, 0:NT * E].rearrange("p (t e) -> p e t", e=E)))
            now = 0
            for sh in (1, 2, 4, 8, 16):
                chain(v.tensor_copy(cnt[:, 1 - now, :, 0:sh], cnt[:, now, :, 0:sh]))
                chain(v.tensor_tensor(cnt[:, 1 - now, :, sh:NT], cnt[:, now, :, sh:NT], cnt[:, now, :, 0:NT - sh],
                                      ALU.add))
                now = 1 - now
            bce = lambda a: a.unsqueeze(2).broadcast_to([P, E, NT])
            more = rt[:, 0, :, :].rearrange("p t e -> p (t e)").rearrange("p (e t) -> p e t", e=E)
            chain(v.tensor_tensor(more, bce(cnt[:, now, :, NT - 1]),
                                  tile128_sb[:, :].unsqueeze(1).broadcast_to([P, E, NT]), ALU.is_gt))
            chain(v.tensor_reduce(small[:, 0, :], more, AX.X, ALU.add))
            at_ = 0
            for sh in (1, 2, 4):
                src, dst = small[:, at_, :], small[:, at_ + 1, :]
                chain(v.tensor_copy(dst[:, 0:sh], src[:, 0:sh]))
                chain(v.tensor_tensor(dst[:, sh:E], src[:, sh:E], src[:, 0:E - sh], ALU.add))
                at_ += 1
            chain(v.tensor_tensor(small[:, 4, :], small[:, 3, :], small[:, 0, :], ALU.subtract))
            chain(v.tensor_scalar(small[:, 4, :], small[:, 4, :], float(P), None, ALU.mult))
            chain(v.tensor_tensor(ends[:, :, :], tiles_sb[:, :].unsqueeze(2).broadcast_to([P, NTILE, E - 1]),
                                  small[:, 3, 0:E - 1].unsqueeze(1).broadcast_to([P, NTILE, E - 1]), ALU.is_ge))
            chain(v.tensor_reduce(expert_f[:, :], ends[:, :, :], AX.X, ALU.add))
            chain(v.tensor_copy(expert[:, :], expert_f[:, :]))
            place = rt[:, 0, :, :]
            chain(v.tensor_tensor(rt[:, 1, :, :], cnt[:, now, :, :].rearrange("p e t -> p t e"),
                                  banks[:, 1, 0:NT * E].rearrange("p (t e) -> p t e", e=E), ALU.subtract))
            chain(v.tensor_tensor(place, rt[:, 1, :, :], banks[:, 0, 0:NT * E].rearrange("p (t e) -> p t e", e=E),
                                  ALU.add))
            chain(v.tensor_tensor(rt[:, 1, :, :], place, small[:, 4, :].unsqueeze(1).broadcast_to([P, NT, E]),
                                  ALU.add))
            for w in range(2):
                chain(v.tensor_tensor(rt[:, 5, :, :], rt[:, 6 + w, :, :], rt[:, 1, :, :], ALU.mult))
                chain(v.tensor_reduce(slot_f[:, w, :], rt[:, 5, :, :], AX.X, ALU.add))
            v.tensor_copy(slot[:, :, :], slot_f[:, :, :]).then_inc(slots_ready, 1)

            def stage_b1(turn, k):
                e = ve.value_load(expert[0:1, bass.ds(turn * TL + k, 1)], min_val=0, max_val=E - 1)
                ve.wait_ge(h_done, turn * TL + (k + 1))
                if not first_use(turn, k):
                    ve.wait_ge(gelu_done, turn * TL + (k - 1))
                by_chunk = lambda a: a.rearrange("p (c n) -> p c n", c=HC)
                v.tensor_tensor(by_chunk(hb[:, k % 2, :]), by_chunk(banks[:, 2 + k % 2, :]),
                                b1_sb[:, bass.ds(e, 1), :].rearrange("p a c -> p (a c)").unsqueeze(2).broadcast_to(
                                    [P, HC, P]), ALU.add).then_inc(hb_ready, 1)

            def stage_y(turn, k):
                e = ve.value_load(expert[0:1, bass.ds(turn * TL + k, 1)], min_val=0, max_val=E - 1)
                ve.wait_ge(y_done, turn * TL + (k + 1))
                v.tensor_tensor(yb[:, k % 2, :], banks[:, 6 + k % 2, 0:D],
                                b2_sb[:, bass.ds(e, 1), :].rearrange("p a n -> p (a n)"), ALU.add).then_inc(y_read, 1)
                if not (isinstance(turn, int) and turn == 0):
                    ve.wait_ge(result_out[k], turn * 16)
                v.tensor_copy(dest[:, k, :], xg[:, k, D + 1:D + 2])
                ve.wait_ge(y_read, turn * TL + (k + 1))
                v.tensor_scalar(ys[:, k, :], yb[:, k % 2, :], xg[:, k, D:D + 1], None, ALU.mult).then_inc(ys_ready, 1)

            pipeline(ve, ((stage_y, 0), (stage_b1, 2)))

            ve.wait_ge(dve, link[0])

            def step6(ins):
                link[0] += 1
                ins.then_inc(dve, 1)

            for b in range(2):
                ve.wait_ge(back_in[b], 32)
                ts = slice(b * NT // 2, (b + 1) * NT // 2)
                chain(v.tensor_tensor(x_sb[:, ts, :], x_sb[:, ts, :], back[b][:, 0, :, :], ALU.add))
                chain(v.tensor_tensor(x_sb[:, ts, :], x_sb[:, ts, :], back[b][:, 1, :, :], ALU.add))
            for t in range(NT):
                step6(v.bn_stats(stats_all[:, t, :], x_sb[:, t, :]))
            ve.wait_ge(dve, link[0])
            sync6 = lambda: ve.wait_ge(dve, link[0])
            moments(stats_all[:, :, :], mean_all[:, :], dev_all[:, :, :], step6, sync6)
            step6(v.tensor_scalar(dev_all[:, 1, :], dev_all[:, 0, :], 1.0 / D, EPS, ALU.mult, ALU.add))
            sync6()
            inverse_root(rstd_all[:, :], dev_all[:, 1, :], dev_all[:, 2, :], step6, sync6)
            for t in range(NT):
                ins = v.tensor_scalar(x_sb[:, t, :], x_sb[:, t, :], mean_all[:, t:t + 1], rstd_all[:, t:t + 1],
                                      ALU.subtract, ALU.mult)
                if t % BT == BT - 1:
                    ins.then_inc(fin_ready, 1)

        @block.gpsimd
        def _(pool):
            pp = nc.gpsimd
            pp.memset(fill[:, 0, :], 0.0).then_inc(fill_set, 1)
            pp.memset(fill[:, 1, :], 1.0).then_inc(fill_set, 1)
            pp.memset(pad[:, :], 0.0).then_inc(iota_done, 1)
            pool.wait_ge(iota_done, 1)
            pp.memset(pad[:, D:D + 1], 0.0).then_inc(iota_done, 1)
            pp.memset(pad[:, D + 1:D + 2], NOWHERE).then_inc(iota_done, 1)
            for e in range(E):
                pp.memset(iota_e[:, e:e + 1], float(e - E)).then_inc(iota_done, 1)
            pp.memset(vx[:, :, :, :, :], 0.0).then_inc(vx_set, 1)
            pool.wait_ge(vx_set, 1)
            pp.memset(vx[:, :, :, :, DK:DK + 1], 1.0).then_inc(vx_set, 1)
            pp.memset(zero[:, :, :], 0.0).then_inc(vx_set, 1)
            for c in range(NCH + 1):
                if c < NCH:
                    i = c % 2
                    if c >= 2:
                        pool.wait_ge(last_done, c - 1)
                    pool.wait_ge(part_done, first_part(c))
                    pp.tensor_tensor(rem[:, i, 1, :, :], rem[:, i, 0, :, :], parts[:, i, 0, :, :],
                                     ALU.subtract).then_inc(rem_done, 1)
                if c >= 1:
                    i = (c - 1) % 2
                    pool.wait_ge(part_done, second_part(c - 1))
                    if c >= 3:
                        pool.wait_ge(stored[i][2], 16 * 2 * ((c - 1) // 2))
                    pp.tensor_tensor(parts[:, i, 2, :, :], rem[:, i, 1, :, :], parts[:, i, 1, :, :],
                                     ALU.subtract).then_inc(last_done, 1)
            pool.wait_ge(v_read, NT // 4)

            def visit(e, r, at):
                if e[0] == "VX":
                    unit = e[1]
                    if unit >= NG:
                        pool.wait_ge(pv_done, at(NB * (unit - 3), NB * NG))
                    pool.wait_ge(vx_set, 3)
                    pp.tensor_copy(vx[:, unit % NG, :, :, 0:DK],
                                   v_sb[:, bass.ds(at(unit // NG * BT, BT), BT),
                                        unit % NG * 32:(unit % NG + 1) * 32].rearrange("p t (h d) -> p t h d", h=GH)
                                   ).then_inc(vx_ready, 1)
                elif e[0] == "SPLIT":
                    unit = e[1]
                    pool.wait_ge(mx_ready, at(unit + 1, NG))
                    by_parity = lambda a: a.rearrange("p (s a) n -> p a s n", a=2)
                    neg, rest = by_parity(mx[:, unit % 2, :, :]), by_parity(mrem[:, unit % 2, :, :])
                    none = by_parity(zero[:, :, :])
                    part = [msp[:, unit % 2, :, j, :, :] for j in range(3)]
                    pp.tensor_tensor(part[0], neg, none, ALU.add).then_inc(msplit, 1)
                    pool.wait_ge(msplit, at(unit * 4 + 1, 4 * NG))
                    pp.tensor_tensor(rest, neg, part[0], ALU.subtract).then_inc(msplit, 1)
                    pool.wait_ge(msplit, at(unit * 4 + 2, 4 * NG))
                    pp.tensor_tensor(part[1], rest, none, ALU.add).then_inc(msplit, 1)
                    pool.wait_ge(msplit, at(unit * 4 + 3, 4 * NG))
                    pp.tensor_tensor(part[2], rest, part[1], ALU.subtract).then_inc(msplit, 1)
                elif e[0] == "QK" and diagonal(e[1] // 2 % NB):
                    i = e[1]
                    pool.wait_ge(exp_done, at(i + 1, 2 * NB * NG))
                    pool.sem_inc(mask_turns, 1)
                    block_ = probs[i % 6][:, :, 0:P]
                    pp.affine_select(out=block_, in_=block_, compare_op=ALU.is_ge, fill=0.0, base=0,
                                     pattern=[[0, 2], [1, P]], channel_multiplier=-1).then_inc(masked, 1)

            walk(pool, visit)

            pool.wait_ge(slots_ready, 1)
            pool.wait_ge(padded, 16)
            for t in range(NT):
                for w in range(2):
                    pp.indirect_dma_start(out=pairs, out_offset=bass.IndirectOffsetOnAxis(ap=slot[:, w, t:t + 1], axis=0),
                                          in_=xr[:, t, w, :], in_offset=None).then_inc(pairs_out, 16)

            bound = pool.to_reg(2 * B * S - 1)

            def stage_out(turn, k):
                pool.wait_ge(ys_ready, turn * TL + (k + 1))
                pool.sem_inc(turns_out, 1)
                pp.indirect_dma_start(out=results, out_offset=bass.IndirectOffsetOnAxis(ap=dest[:, k, :], axis=0),
                                      in_=ys[:, k, :], in_offset=None, bounds_check=bound,
                                      oob_is_err=False).then_inc(result_out[k], 16)

            pipeline(pool, ((stage_out, 0),))


def first_use(turn, k):
    return isinstance(turn, int) and turn == 0 and k < 2


def pipeline(eng, stages):
    lead = max(n for _, n in stages)
    turns = NTILE // TL
    for t in range(-lead, 0):
        for stage, n in stages:
            if 0 <= t + n:
                stage(0, t + n)
    def whole(turn):
        for k in range(TL):
            for stage, n in stages:
                stage(turn + (k + n) // TL, (k + n) % TL)

    whole(0)
    with eng.Fori(1, turns - 1) as turn:
        whole(turn)
    for k in range(TL):
        for stage, n in stages:
            if k + n < TL:
                stage(turns - 1, k + n)


def kernel(L0_attn_x, L0_attn_W_Q, L0_attn_W_K, L0_attn_W_V, L0_attn_W_O, L0_ffn_Wg, L0_ffn_bg,
           L0_ffn_W1, L0_ffn_b1, L0_ffn_W2, L0_ffn_b2):
    import concourse.bacc as bacc
    from concourse.bass_utils import run_bass_kernel_spmd

    f = lambda a: np.asarray(a)
    x = f(L0_attn_x).reshape(B * S, D)
    flip = np.arange(D).reshape(H, 2, DK // 2)[:, ::-1].reshape(-1)
    WQ, WK = f(L0_attn_W_Q), f(L0_attn_W_K)
    theta = (np.float32(1.0) / np.float32(10000.0) ** (np.arange(0, DK, 2, dtype=np.float32) / np.float32(DK)))
    ang = np.outer(np.arange(S, dtype=np.float32), theta.astype(np.float32)).astype(np.float32)
    ang = np.concatenate([ang, ang], axis=-1)
    sign = np.where(np.arange(DK) < DK // 2, -1.0, 1.0).astype(np.float32)
    cosT = np.tile(np.cos(ang).T, (H, 1)).astype(np.float32)
    sinT = np.tile((np.sin(ang) * sign).T, (H, 1)).astype(np.float32)
    q, k = np.arange(P)[:, None], np.arange(P)[None, :]
    mask_a = np.where(k > q, np.float32(-1e30), np.float32(0.0))
    arrays = {
        "xT": x.T, "x": x,
        "w": np.stack([WQ.T, WQ[flip].T, WK.T, WK[flip].T, f(L0_attn_W_V).T, f(L0_attn_W_O).T], axis=1),
        "wg": f(L0_ffn_Wg), "bg": f(L0_ffn_bg),
        "w1": f(L0_ffn_W1), "b1": f(L0_ffn_b1).reshape(E, HC, P).transpose(2, 0, 1), "w2": f(L0_ffn_W2), "b2": f(L0_ffn_b2),
        "cs": np.stack([cosT, sinT], axis=1), "ident": np.eye(P, dtype=np.float32),
        "maskA": mask_a,
        "before": np.stack([q < k, np.ones((P, P))], axis=1).astype(np.float32),
        "tile128": np.tile(np.arange(NT, dtype=np.float32) * P, (P, 1)),
        "tokens": np.stack([q + P * np.arange(NT), q + P * np.arange(NT) + B * S], axis=1).astype(np.float32),
        "tiles": np.tile(np.arange(NTILE, dtype=np.float32), (P, 1)),
    }
    arrays = {n: np.ascontiguousarray(a) for n, a in arrays.items()}
    nc = bacc.Bacc("TRN2", target_bir_lowering=False, num_devices=1)
    args = {n: nc.dram_tensor(f"in_{n}", a.shape, mybir.dt.from_np(a.dtype), kind="ExternalInput").ap()
            for n, a in arrays.items()}
    out = nc.dram_tensor("out_0", (B * S, D), F32, kind="ExternalOutput").ap()
    build(nc, out=out, **args)
    r = run_bass_kernel_spmd(nc, [{f"in_{n}": a for n, a in arrays.items()}], core_ids=[0])
    return r.results[0]["out_0"].reshape(B, S, D)
```

```python
from contextlib import ExitStack

import numpy as np
import concourse.bass as bass
from concourse import mybir

F32 = mybir.dt.float32
BF16 = mybir.dt.bfloat16
ALU = mybir.AluOpType
ACT = mybir.ActivationFunctionType
AX = mybir.AxisListType

P = 128
B, S, D = 4, 1024, 128
H, DK = 16, 8
E, HID = 8, 512
NT = B * S // P
BT = S // P
GH = 4
NG = H // GH
CH = 512
NCH = B * S // CH
HC = HID // P
ROWS = 56
MROW = 32
Q_PLACES = ((0, (0, 3, 6)), (1, (1, 2)), (2, (5,)))
K_PLACES = ((0, (1, 3, 5)), (1, (0, 2)), (2, (6,)))
SCALE = float(np.float32(1.0) / np.sqrt(np.float32(DK)))
EPS = 1e-5
GATE_EPS = 1e-8
TL = 8
NTILE = -(-(2 * B * S // P + E - 1) // TL) * TL
CAPT = B * S // P + 1
SPARE = NTILE - 2 * B * S // P
ROW = D + 4
NOWHERE = float(1 << 20)
RING = 3


def pass_a_items():
    items = []
    for sb in range(BT):
        whole, rest = divmod((sb + 1) * P, CH)
        parts = [(CH * i, CH) for i in range(whole)] + ([(CH * whole, rest)] if rest else [])
        for t0, n in parts:
            masked = t0 + n == (sb + 1) * P
            if 2 * n <= CH:
                items += [(par, sb, t0, n, (0, 1), masked) for par in (0, 1)]
            else:
                items += [(par, sb, t0, n, (slot,), masked) for slot in (0, 1) for par in (0, 1)]
    return items


def pass_b_steps():
    steps = []
    for c in range(S // CH):
        for j in range((c + 1) * CH // P):
            s0 = max(P * j, CH * c)
            steps.append((c, j, s0, CH * (c + 1) - s0))
    return steps


A_ITEMS = pass_a_items()
B_STEPS = pass_b_steps()
NA, NB = len(A_ITEMS), len(B_STEPS)
NU = B * NG
C_LAST = [max(k for k, st in enumerate(B_STEPS) if st[0] == c) for c in range(2)]
A_LEAD, A_END = 7, 6


def diagonal(k):
    c, j, s0, n = B_STEPS[k]
    return s0 == P * j


DIAG = [sum(diagonal(i) for i in range(k + 1)) for k in range(NB)]


def a_quota():
    steps = [k % NB for k in range(A_LEAD, NB + A_END + 1)]
    work = [B_STEPS[k][3] for k in steps]
    return [NA * sum(work[:i + 1]) // sum(work) for i in range(len(work))]


def schedule():
    quota = a_quota()
    ev = []
    ev.append(("VX", 0))
    ev += [("A", 0, i) for i in range(NA)] + [("SPLIT", 0)]
    lead = NB - A_LEAD
    ev += [("A", 1, i) for i in range(quota[lead - 1])]
    ev.insert(len(ev) - quota[lead - 1] // 2, ("MT", 0))
    ev.insert(len(ev) - quota[lead - 1] // 2, ("MROWS", 0))
    ev += [("QK", 0), ("QK", 1)]

    def after(bt):
        order = [
            [("T1", bt, 0)], [("T1", bt, 1)], [("WO", bt, 0)], [("WO", bt, 1)],
            [("LNM", bt, 0)], [("LNM", bt, 1)], [("LNV", bt, 0)], [("LNR", bt, 0)], [("LNR", bt, 1)],
            [("LNA", bt, 0)], [("LNA", bt, 1)], [("T2", bt, 0)], [("T2", bt, 1), ("XC", bt)], [("LG", bt)],
            [("RA", bt, 0)], [("RX", bt), ("RS", bt, 0)], [("RB", bt, 0)], [("RB", bt, 1)],
            [("RC", bt, 0)], [("RC", bt, 1)], [("RK", bt)], [("RD", bt, 0)], [("RD", bt, 1)],
            [("RE", bt, 0)], [("RE", bt, 1)], [("RF", bt, 0)], [("RF", bt, 1)],
        ] + [[("SC", bt, i), ("SC", bt, i + 1)] for i in range(0, 2 * BT, 2)]
        if bt < B - 1:
            order += [[], [("SW", bt)]]
        return {3 + i: events for i, events in enumerate(order)}

    for u in range(NU):
        for k in range(NB):
            step = u * NB + k
            if k >= A_LEAD:
                v, i = u + 2, k - A_LEAD
            else:
                v, i = u + 1, k + NB - A_LEAD
            items = []
            if v < NU and not (v == 1 and i < lead):
                items = [("A", v, n) for n in range(quota[i - 1] if i else 0, quota[i])]
            half = len(items) // 2
            if k == 5 and u % NG == 3:
                ev.append(("MARK", u))
            if step + 1 < NU * NB:
                ev.append(("QK", 2 * step + 2))
            ev += items[:half]
            if step + 1 < NU * NB:
                ev.append(("QK", 2 * step + 3))
            ev += items[half:]
            if k == A_END and u + 1 < NU:
                ev.append(("SPLIT", u + 1))
            if step:
                ev.append(("PV", step - 1))
                if (step - 1) % NB in C_LAST:
                    ev.append(("EV", 2 * ((step - 1) // NB) + C_LAST.index((step - 1) % NB)))
            for back in (0, 1):
                if step >= 3 and (step - 3) % NB == C_LAST[back]:
                    ev.append(("OT", 2 * ((step - 3) // NB) + back))
            if k == 2 and u + 2 < NU:
                ev.append(("LOAD", u + 2))
            if k == 5 and u + 1 < NU:
                ev.append(("VX", u + 1))
            if k == A_END + 1 and u + 1 < NU:
                ev += [("MT", u + 1), ("MROWS", u + 1)]
            if u >= NG:
                ev += after(u // NG - 1).get(u % NG * NB + k, [])
    last = NU * NB - 1
    ev += [("PV", last), ("EV", 2 * NU - 1), ("OT", 2 * NU - 1)]
    for _, events in sorted(after(B - 1).items()):
        ev += events
    r, out = 0, []
    for e in ev:
        if e[0] in ("A", "MT", "OT", "T1", "WO", "T2", "LG", "RK"):
            out.append((e, r))
            r += 1
        else:
            out.append((e, None))
    return out, r


EVENTS, RING_TOTAL = schedule()
RING_OF = {e: r for e, r in EVENTS if r is not None}
MARKS = [i for i, (e, r) in enumerate(EVENTS) if e[0] == "MARK"]
TURNS = B - 2
PROLOGUE, BODY, EPILOGUE = EVENTS[:MARKS[0]], EVENTS[MARKS[0]:MARKS[1]], EVENTS[MARKS[TURNS]:]
RING_BATCH = sum(r is not None for _, r in BODY)
STRIDE = {"A": NG, "SPLIT": NG, "MT": NG, "MROWS": NG, "LOAD": NG, "VX": NG, "MARK": NG, "QK": 2 * NB * NG,
          "PV": NB * NG, "EV": 2 * NG, "OT": 2 * NG}
STRIDE.update({kind: 1 for kind in ("T1", "WO", "LNM", "LNV", "LNR", "LNA", "T2", "LG", "XC", "RA", "RX", "RS",
                                    "RB", "RC", "RK", "RD", "RE", "RF", "SC", "SW")})
assert RING_BATCH % RING == 0
for turn in range(1, TURNS):
    moved = [((e[0], e[1] + turn * STRIDE[e[0]]) + e[2:], r if r is None else r + turn * RING_BATCH) for e, r in BODY]
    assert moved == EVENTS[MARKS[turn]:MARKS[turn + 1]]


def first_part(c):
    return max(1, 2 * c)


def second_part(c):
    return 2 * c + 3 if c < NCH - 1 else 2 * NCH


def walk(eng, visit):
    static = lambda n, stride: n
    for e, r in PROLOGUE:
        visit(e, r, static)
    with eng.Fori(0, TURNS) as turn:
        for e, r in BODY:
            visit(e, r, lambda n, stride: turn * stride + n)
    for e, r in EPILOGUE:
        visit(e, r, static)


def build(nc, xT, x, w, wg, bg, w1, b1, w2, b2,
          cs, ident, maskA, before, tile128, tokens, tiles, first_row, out):
    ctx = ExitStack()
    with ctx:
        def sb(name, shape, dt=F32):
            return ctx.enter_context(nc.sbuf_tensor(name, shape, dt))

        def sem(name):
            return ctx.enter_context(nc.semaphore(name))

        stack = nc.dram_tensor("stack", [2, B, ROWS // 8, H, 8, S], BF16, kind="Internal").ap()
        pairs = nc.dram_tensor("pairs", [(E * CAPT + SPARE) * P, ROW], F32, kind="Internal").ap()
        results = nc.dram_tensor("results", [2 * B * S, D], F32, kind="Internal").ap()

        xT_sb = sb("xT_sb", [P, B * S])
        x_sb = sb("x_sb", [P, NT, D])
        w_sb = sb("w_sb", [P, 6, D])
        wg_sb = sb("wg_sb", [P, E])
        bg_sb = sb("bg_sb", [P, E])
        w1_sb = sb("w1_sb", [P, E, HID])
        w2_sb = sb("w2_sb", [P, E, HC, D])
        b1_sb = sb("b1_sb", [P, E, HC])
        b2_sb = sb("b2_sb", [P, E, D])
        cs_sb = sb("cs_sb", [P, 2, S])
        id_sb = sb("id_sb", [P, P])
        idb_sb = sb("idb_sb", [P, P], BF16)
        mask_sb = sb("mask_sb", [P, 2, P], BF16)
        mask_f = sb("mask_f", [P, P])
        fill = sb("fill", [P, 2, S], BF16)
        v_sb = sb("v_sb", [P, NT, D])
        attn = sb("attn", [P, BT, D])
        region = sb("region", [P, 16384])
        logits = sb("logits", [P, BT, E])
        rt = xT_sb[:, 0:9 * BT * E].rearrange("p (k t e) -> p k t e", k=9, t=BT)
        xr = xT_sb[:, 9 * BT * E:9 * BT * E + 2 * BT * ROW].rearrange("p (t k n) -> p t k n", t=BT, k=2)
        r1 = sb("r1", [P, 8, BT])
        iota_e = sb("iota_e", [P, E])
        before_sb = sb("before_sb", [P, 2, P])
        tile128_sb = sb("tile128_sb", [P, NT])
        tokens_sb = sb("tokens_sb", [P, 2, NT])
        tiles_sb = sb("tiles_sb", [P, NTILE])
        first_row_sb = sb("first_row_sb", [P, E])
        next_row = sb("next_row", [P, E])
        ranks = sb("ranks", [P, 2, BT, E])
        cnt = sb("cnt", [P, 2, E, BT])
        small = sb("small", [P, 6, E])
        ends = sb("ends", [P, NTILE, E])
        expert_f = sb("expert_f", [P, 2, NTILE])
        expert = sb("expert", [P, NTILE], mybir.dt.int32)
        tile_at = sb("tile_at", [P, NTILE], mybir.dt.int32)
        slot_f = sb("slot_f", [P, 2, BT])
        slot = sb("slot", [P, 2, BT], mybir.dt.uint32)
        pad_row = sb("pad_row", [P, E], mybir.dt.int32)
        pad = sb("pad", [P, ROW])
        dest = sb("dest", [P, TL, 1], mybir.dt.uint32)

        flat = lambda a: a.rearrange("p a n -> p (a n)")
        rot = flat(w1_sb[:, :, :]).rearrange("p (b t w n) -> p b t w n", b=2, t=2, w=2)
        rem = w2_sb[:, :, :, :].rearrange("p e c n -> p (e c n)").rearrange(
            "p (b t w n) -> p b t w n", b=2, t=2, w=2)
        parts = flat(x_sb[:, :, :])[:, 0:3072].bitcast(BF16).rearrange("p (b j w n) -> p b j w n", b=2, j=3, w=2)
        qst = region[:, 0:4096].bitcast(BF16).rearrange("p (g s n) -> p g s n", g=NG, s=2)
        kst = region[:, 4096:8192].bitcast(BF16).rearrange("p (g s n) -> p g s n", g=NG, s=2)
        probs = [a[:, i, :, :] for a, n in ((region[:, 8192:12288], 4),
                                            (cs_sb[:, :, :].rearrange("p a n -> p (a n)"), 2))
                 for a in (a.rearrange("p (k w n) -> p k w n", k=n, w=2),) for i in range(n)]
        vx = region[:, 12288:16384].rearrange("p (g t h c) -> p g t h c", g=NG, t=BT, h=GH)
        ot = sb("ot", [P, 2, CH])
        rden = sb("rden", [P, 2, 4 * GH])
        mx = sb("mx", [P, 2, GH, BT])
        mx2 = sb("mx2", [P, 2, GH, BT // 2])
        mrem = sb("mrem", [P, 2, GH, BT])
        zero = sb("zero", [P, GH, BT])
        msp = sb("msp", [P, 2, 2, 3, 2, BT], BF16)
        mparts = sb("mparts", [GH * 3 * BT, 2, P], BF16)
        aT = sb("aT", [P, 2, CH])
        y1 = sb("y1", [P, 2, 4, D])
        nwt = sb("nwt", [P, BT])
        xg = region[:, 13568:13568 + TL * ROW].rearrange("p (b n) -> p b n", b=TL)
        xgT = region[:, 0:256].rearrange("p (b n) -> p b n", b=2)
        hb = region[:, 256:1280].rearrange("p (b n) -> p b n", b=2)
        hg = region[:, 1280:2304].rearrange("p (b n) -> p b n", b=2)
        w1e = region[:, 2304:3328].rearrange("p (b n) -> p b n", b=2)
        yb = region[:, 3328:3584].rearrange("p (b n) -> p b n", b=2)
        ys = region[:, 3584:4608].rearrange("p (b n) -> p b n", b=TL)
        back = [a[:, i * 2 * BT * D:(i + 1) * 2 * BT * D].rearrange("p (k t n) -> p k t n", k=2, n=D)
                for a in (xT_sb[:, :], region[:, 0:4096]) for i in range(2)]
        stats = sb("stats", [P, BT, 6])
        mean = sb("mean", [P, BT])
        dev = sb("dev", [P, 3, BT])
        rstd = sb("rstd", [P, BT])
        stats_all = sb("stats_all", [P, NT, 6])
        mean_all = sb("mean_all", [P, NT])
        dev_all = sb("dev_all", [P, 3, NT])
        rstd_all = sb("rstd_all", [P, NT])
        shift_all = sb("shift_all", [P, NT])

        banks = ctx.enter_context(nc.psum_tensor("banks", [P, 8, CH], F32))
        ring = banks[:, 0:RING, :]
        score = banks[:, RING:RING + 4, :].rearrange("p (k w) n -> p k w n", k=2)
        pv = banks[:, RING + 4, :]

        weights_in = sem("weights_in")
        xT_in = [sem(f"xT_in{b}") for b in range(B)]
        loads = sem("loads")
        x_in = sem("x_in")
        late_in = sem("late_in")
        fill_set = sem("fill_set")
        stacks_clear = sem("stacks_clear")
        masks_ready = sem("masks_ready")
        fills = sem("fills")
        proj_done = sem("proj_done")
        proj_read = sem("proj_read")
        rotated = sem("rotated")
        part_done = sem("part_done")
        rem_done = sem("rem_done")
        last_done = sem("last_done")
        stored = [[sem(f"stored{i}_{part}") for part in range(3)] for i in range(2)]
        v_done = sem("v_done")
        v_read = sem("v_read")
        vx_set = sem("vx_set")
        dma_unit = [sem(f"unit_loaded{g}") for g in range(NG)]
        vx_ready = sem("vx_ready")
        ring_full = sem("ring_full")
        ring_read = sem("ring_read")
        mx_ready = sem("mx_ready")
        msplit = sem("msplit")
        mrows = [sem(f"mrows{i}") for i in range(2)]
        qk_done = sem("qk_done")
        exp_done = sem("exp_done")
        pv_done = sem("pv_done")
        ot_ready = sem("ot_ready")
        rden_ready = sem("rden_ready")
        masked = sem("masked")
        pool_turns = sem("pool_turns")
        dve = sem("dve")
        ln = sem("ln")
        x1_done = sem("x1_done")
        x1_copied = sem("x1_copied")
        xr_free = sem("xr_free")
        iota_done = sem("iota_done")
        top_in = sem("top_in")
        top_exp = sem("top_exp")
        top_mask = sem("top_mask")
        route = sem("route")
        spare_in = sem("spare_in")
        pad_ready = sem("pad_ready")
        tiles_ready = sem("tiles_ready")
        slots_ready = sem("slots_ready")
        pairs_out = sem("pairs_out")
        pair_in = [sem(f"pair_in{k}") for k in range(TL)]
        xg_turned = sem("xg_turned")
        xgT_ready = sem("xgT_ready")
        h_done = sem("h_done")
        hb_ready = sem("hb_ready")
        gelu_done = sem("gelu_done")
        w1e_ready = sem("w1e_ready")
        y_done = sem("y_done")
        y_read = sem("y_read")
        ys_ready = sem("ys_ready")
        result_out = [sem(f"result_out{k}") for k in range(TL)]
        back_in = [sem(f"back_in{k}") for k in range(B)]
        first_added = sem("first_added")
        scales_ready = sem("scales_ready")
        fin_ready = sem("fin_ready")
        last_ready = sem("last_ready")
        out_done = sem("out_done")

        N_LOADS = 11
        block = ctx.enter_context(nc.Block())

        @block.sync
        def _(sp):
            sp.dma_start(w_sb[:, :, :], w).then_inc(weights_in, 16)
            for b in range(B):
                sp.dma_start(xT_sb[:, b * S:(b + 1) * S], xT[:, b * S:(b + 1) * S]).then_inc(xT_in[b], 16)
                if b == 0:
                    sp.dma_start(cs_sb[:, :, :], cs).then_inc(weights_in, 16)
                    sp.wait_ge(fill_set, 2)
                    for w_ in range(2):
                        sp.dma_start(stack[w_, :, MROW // 8].rearrange("b h r n -> (h r) b n"),
                                     fill[:, w_:w_ + 1, :].broadcast_to([P, B, S])).then_inc(fills, 16)
            sp.dma_start(id_sb[:, :], ident).then_inc(loads, 16)
            sp.dma_start(mask_f[:, :], maskA).then_inc(loads, 16)
            sp.dma_start(wg_sb[:, :], wg).then_inc(loads, 16)
            sp.dma_start(bg_sb[:, :], bg.partition_broadcast(P)).then_inc(loads, 16)
            sp.dma_start(before_sb[:, :, :], before).then_inc(loads, 16)
            sp.dma_start(tile128_sb[:, :], tile128).then_inc(loads, 16)
            sp.dma_start(tokens_sb[:, :, :], tokens).then_inc(loads, 16)
            sp.dma_start(tiles_sb[:, :], tiles).then_inc(loads, 16)
            sp.dma_start(first_row_sb[:, :], first_row).then_inc(loads, 16)
            sp.dma_start(b1_sb[:, :, :], b1).then_inc(loads, 16)
            sp.dma_start(b2_sb[:, :, :], b2.partition_broadcast(P)).then_inc(loads, 16)

            def store(c, part):
                b, i = divmod(c, 2)
                for w_, places in ((0, Q_PLACES), (1, K_PLACES)):
                    blocks = places[part][1]
                    step = blocks[1] - blocks[0] if len(blocks) > 1 else 1
                    sp.dma_start(stack[w_, b, blocks[0]:blocks[-1] + 1:step, :, :, i * CH:(i + 1) * CH]
                                 .rearrange("z h r n -> (h r) z n"),
                                 parts[:, i, part, w_, :].unsqueeze(1).broadcast_to([P, len(blocks), CH])
                                 ).then_inc(stored[i][part], 16)

            sp.wait_ge(stacks_clear, 1)

            def load_unit(b, g):
                for w_, dst in ((0, qst), (1, kst)):
                    for par in (0, 1):
                        for slot_ in (0, 1):
                            src = stack[w_, bass.ds(b, 1), :, GH * g + 2 * slot_ + par, :, :]
                            sp.dma_start(dst[64 * par:64 * par + ROWS, g, slot_, :],
                                         src.rearrange("o z r n -> (o z) r n")).then_inc(dma_unit[g], 16)

            for c in range(NCH + 1):
                if c < NCH:
                    sp.wait_ge(part_done, first_part(c))
                    store(c, 0)
                if c >= 1:
                    sp.wait_ge(part_done, second_part(c - 1))
                    store(c - 1, 1)
                    sp.wait_ge(last_done, c)
                    store(c - 1, 2)
                if c == 3:
                    sp.wait_ge(fills, 16 * 2)
                    for i in range(2):
                        for part in range(3):
                            sp.wait_ge(stored[i][part], 16 * 2)
                    load_unit(0, 0)
            load_unit(0, 1)

            sp.sem_inc(xr_free, 1)

            def visit(e, r, at):
                if e[0] == "SW":
                    sp.wait_ge(pairs_out, at(16 * 2 * BT * (e[1] + 1), 16 * 2 * BT))
                    sp.sem_inc(xr_free, 1)
                elif e[0] == "LOAD":
                    v = e[1]
                    if v >= NG:
                        sp.wait_ge(qk_done, at(2 * NB * (v - 3), 2 * NB * NG))
                    load_unit(at(v // NG, 1), v % NG)
                    if v == 3:
                        sp.wait_ge(last_done, NCH)
                        sp.dma_start(w1_sb[:, :, :], w1.rearrange("e p n -> p e n")).then_inc(late_in, 16)
                        sp.dma_start(w2_sb[:, :, :, :], w2.rearrange("e (c p) n -> p e c n", p=P)
                                     ).then_inc(late_in, 16)
                elif e[0] == "MROWS":
                    v = e[1]
                    sp.wait_ge(ring_read, at(RING_OF[("MT", v)] + 1, RING_BATCH))
                    for par in (0, 1):
                        sp.dma_start(qst[64 * par + MROW:64 * par + MROW + 3, v % NG, :, :],
                                     mparts[par * 6 * BT:(par + 1) * 6 * BT, v % 2, :]).then_inc(mrows[v % 2], 16)
                    if v == 0:
                        for i in range(2):
                            for part in range(3):
                                sp.wait_ge(stored[i][part], 16 * 2 * (NCH // 2))
                        sp.dma_start(x_sb[:, :, :], x.rearrange("(t p) n -> p t n", p=P)).then_inc(x_in, 16)
                    elif v == 1:
                        sp.wait_ge(iota_done, 3)
                        sp.dma_start(pairs[E * CAPT * P:, :].rearrange("(t p) n -> p t n", p=P),
                                     pad[:, :].unsqueeze(1).broadcast_to([P, SPARE, ROW])).then_inc(spare_in, 16)

            walk(sp, visit)
            sp.wait_ge(pad_ready, 1)
            for e_ in range(E):
                row = sp.value_load(pad_row[0:1, e_:e_ + 1], min_val=0, max_val=(E * CAPT - 1) * P)
                sp.dma_start(pairs[bass.ds(row, P), :], pad[:, :]).then_inc(spare_in, 16)

            sp.wait_ge(tiles_ready, 1)
            sp.wait_ge(spare_in, 16 * (1 + E))
            sp.wait_ge(pairs_out, 16 * 2 * NT)

            def load_pairs(turn, k):
                t = sp.value_load(tile_at[0:1, bass.ds(turn * TL + k, 1)], min_val=0, max_val=E * CAPT + SPARE - 1)
                if not isinstance(turn, int):
                    sp.wait_ge(ys_ready, turn * TL + (k + 1 - TL))
                sp.dma_start(xg[:, k, :], pairs.rearrange("(t p) n -> t p n", p=P)[bass.ds(t, 1)]
                             .rearrange("o p n -> p (o n)")).then_inc(pair_in[k], 16)

            for k in range(TL):
                load_pairs(0, k)
            with sp.Fori(1, NTILE // TL) as turn:
                for k in range(TL):
                    load_pairs(turn, k)
            for k in range(TL):
                sp.wait_ge(result_out[k], 16 * (NTILE // TL))
            for b in range(B):
                for k in range(2):
                    sp.dma_start(back[b][:, k, :, :], results[k * B * S + b * S:k * B * S + (b + 1) * S, :]
                                 .rearrange("(t p) n -> p t n", p=P)).then_inc(back_in[b], 16)
            for b in range(B):
                if b < B - 1:
                    sp.wait_ge(fin_ready, b + 1)
                else:
                    sp.wait_ge(last_ready, 1)
                sp.dma_start(out.rearrange("(b t p) n -> b p t n", b=B, p=P)[b], x_sb[:, b * BT:(b + 1) * BT, :]
                             ).then_inc(out_done, 16)
            sp.wait_ge(out_done, 16 * B)

        @block.tensor
        def _(pe):
            mm = nc.tensor.matmul
            pe.wait_ge(weights_in, 32)
            for c in range(NCH):
                bank = 4 * (c % 2)
                if c % 2 == 0:
                    pe.wait_ge(xT_in[c // 2], 16)
                if c >= 2:
                    pe.wait_ge(proj_read, c - 1)
                for i, w in enumerate((0, 2, 1, 3)):
                    last = mm(banks[:, bank + i, :], w_sb[:, w, :], xT_sb[:, c * CH:(c + 1) * CH],
                              start=True, stop=True)
                last.then_inc(proj_done, 1)
            for c in range(NT // 4):
                pe.wait_ge(proj_read, NCH - 1 if c < 4 else NCH)
                for t in range(4):
                    tile = 4 * c + t
                    last = mm(banks[:, c, t * P:(t + 1) * P], xT_sb[:, tile * P:(tile + 1) * P],
                              w_sb[:, 4, :], start=(t == 0), stop=True, skip_group_check=True)
                last.then_inc(v_done, 1)

            pe.wait_ge(masks_ready, 2)
            pe.wait_ge(v_read, RING)

            def visit(e, r, at):
                kind = e[0]
                if r is not None and r >= RING:
                    pe.wait_ge(ring_read, at(r - RING + 1, RING_BATCH))
                bank = None if r is None else r % RING
                if kind == "A":
                    v, i = e[1:]
                    if i == 0:
                        pe.wait_ge(dma_unit[v % NG], at(128 * (v // NG + 1), 128))
                    par, sb_, t0, n, slots, is_masked = A_ITEMS[i]
                    rows = slice(64 * par, 64 * par + 64)
                    for m, slot_ in enumerate(slots):
                        last = mm(ring[:, bank, m * n:(m + 1) * n], qst[rows, v % NG, slot_, sb_ * P:(sb_ + 1) * P],
                                  kst[rows, v % NG, slot_, t0:t0 + n], start=(m == 0), stop=not is_masked,
                                  skip_group_check=True)
                    if is_masked:
                        k = len(slots)
                        view = ring[:, bank, 0:k * n].rearrange("p (k n) -> p k n", k=k)[:, :, n - P:n]
                        last = mm(view, idb_sb[:, :], mask_sb[:, 0:k, :], start=False, stop=True,
                                  skip_group_check=True)
                    last.then_inc(ring_full, 1)
                elif kind == "MT":
                    v = e[1]
                    pe.wait_ge(msplit, at(4 * (v + 1), 4 * NG))
                    nc.tensor.transpose(ring[0:GH * 3 * BT, bank, 0:P // 2].bitcast(BF16),
                                        msp[:, v % 2, :, :, :, :].rearrange("p a j s n -> p (a j s n)"),
                                        idb_sb[:, :]).then_inc(ring_full, 1)
                elif kind == "QK":
                    i = e[1]
                    u, k = divmod(i // 2, NB)
                    c, j, s0, n = B_STEPS[k]
                    slot_ = i % 2
                    if i == 0:
                        pe.wait_ge(v_read, NT // 4)
                    if k == 0 and slot_ == 0:
                        pe.wait_ge(mrows[u % 2], at(32 * (u // 2 + 1), 32 * NG // 2))
                    if i >= 2:
                        pe.wait_ge(exp_done, at(i - 1, 2 * NB * NG))
                    for par in (0, 1):
                        rows = slice(64 * par, 64 * par + 64)
                        last = mm(score[:, slot_, par, 0:n], kst[rows, u % NG, slot_, j * P:(j + 1) * P],
                                  qst[rows, u % NG, slot_, s0:s0 + n], start=True, stop=True)
                    last.then_inc(qk_done, 1)
                elif kind == "PV":
                    u, k = divmod(e[1], NB)
                    c, j, s0, n = B_STEPS[k]
                    if k == 0:
                        pe.wait_ge(vx_ready, at(u + 1, NG))
                    if j == 0 and 2 * u + c > 0:
                        pe.wait_ge(ot_ready, at(2 * u + c, 2 * NG))
                    if diagonal(k):
                        pe.wait_ge(masked, at(2 * (u * DIAG[-1] + DIAG[k]), 2 * NG * DIAG[-1]))
                    else:
                        pe.wait_ge(exp_done, at(2 * e[1] + 2, 2 * NB * NG))
                    for slot_ in (0, 1):
                        for par in (0, 1):
                            h = 2 * slot_ + par
                            last = mm(pv[32 * h:32 * h + 32, s0 - c * CH:s0 - c * CH + n],
                                      vx[:, u % NG, j, h, :], probs[(2 * e[1] + slot_) % 6][:, par, 0:n],
                                      start=(j == 0), stop=(k == C_LAST[c]),
                                      tile_position=(0, 32 * h), skip_group_check=True)
                    last.then_inc(pv_done, 1)
                elif kind == "OT":
                    n = e[1]
                    pe.wait_ge(ot_ready, at(n + 1, 2 * NG))
                    for t in range(4):
                        last = nc.tensor.transpose(ring[:, bank, t * P:(t + 1) * P],
                                                   ot[:, n % 2, t * P:(t + 1) * P], id_sb[:, :])
                    last.then_inc(ring_full, 1)
                elif kind == "LG":
                    bt = e[1]
                    for c in range(2):
                        pe.wait_ge(ring_read, at(RING_OF[("T2", bt, c)] + 1, RING_BATCH))
                        for t in range(4):
                            last = mm(ring[:, bank, (4 * c + t) * E:(4 * c + t + 1) * E],
                                      aT[:, c, t * P:(t + 1) * P], wg_sb[:, :],
                                      start=(c == t == 0), stop=True, skip_group_check=True)
                    last.then_inc(ring_full, 1)
                elif kind == "RK":
                    pe.wait_ge(top_mask, at(e[1] + 1, 1))
                    for k in range(2):
                        last = mm(ring[:, bank, k * BT * E:(k + 1) * BT * E], before_sb[:, k, :], rt[:, 4, :, :],
                                  start=(k == 0), stop=True, skip_group_check=True)
                    last.then_inc(ring_full, 1)
                elif kind in ("T1", "WO", "T2"):
                    bt, c = e[1:]
                    if kind == "T1":
                        pe.wait_ge(ring_read, at(RING_OF[("OT", 2 * NG * bt + 2 * NG - 1)] + 1, RING_BATCH))
                    elif kind == "WO":
                        pe.wait_ge(ring_read, at(RING_OF[("T1", bt, c)] + 1, RING_BATCH))
                    else:
                        pe.wait_ge(x1_done, at(2 * bt + c + 1, 2))
                    for t in range(4):
                        cols = slice(t * P, (t + 1) * P)
                        if kind == "T1":
                            last = nc.tensor.transpose(ring[:, bank, cols], attn[:, 4 * c + t, :], id_sb[:, :])
                        elif kind == "WO":
                            last = mm(ring[:, bank, cols], aT[:, c, cols], w_sb[:, 5, :], start=(t == 0), stop=True,
                                      skip_group_check=True)
                        else:
                            last = nc.tensor.transpose(ring[:, bank, cols], xr[:, 4 * c + t, 0, 0:D], id_sb[:, :])
                    last.then_inc(ring_full, 1)

            walk(pe, visit)
            pe.wait_ge(ring_read, RING_TOTAL)

            pe.wait_ge(tiles_ready, 1)
            pe.wait_ge(late_in, 32)

            def stage_down(turn, k):
                e = pe.value_load(expert[0:1, bass.ds(turn * TL + k, 1)], min_val=0, max_val=E - 1)
                pe.wait_ge(gelu_done, turn * TL + (k + 1))
                if not first_use(turn, k):
                    pe.wait_ge(y_read, turn * TL + (k - 1))
                for hc in range(HC):
                    last = mm(banks[:, 6 + k % 2, 0:D], hg[:, k % 2, hc * P:(hc + 1) * P],
                              w2_sb[:, bass.ds(e, 1), hc, :].rearrange("p a n -> p (a n)"),
                              start=(hc == 0), stop=(hc == HC - 1))
                last.then_inc(y_done, 1)

            def stage_up(turn, k):
                pe.wait_ge(w1e_ready, turn * TL + (k + 1))
                pe.wait_ge(xgT_ready, turn * TL + (k + 1))
                if not first_use(turn, k):
                    pe.wait_ge(hb_ready, turn * TL + (k - 1))
                for hc in range(HC):
                    last = mm(banks[:, 2 + k % 2, hc * P:(hc + 1) * P], w1e[:, k % 2, hc * P:(hc + 1) * P],
                              xgT[:, k % 2, :], start=(hc == 0), stop=(hc == HC - 1), skip_group_check=True)
                last.then_inc(h_done, 1)

            def stage_tx(turn, k):
                pe.wait_ge(pair_in[k], turn * 16 + 16)
                if not first_use(turn, k):
                    pe.wait_ge(xgT_ready, turn * TL + (k - 1))
                nc.tensor.transpose(banks[:, k % 2, 0:P], xg[:, k, 0:D], id_sb[:, :]).then_inc(xg_turned, 1)

            pipeline(pe, ((stage_down, 0), (stage_up, 2), (stage_tx, 3)))

        @block.scalar
        def _(act):
            for c in range(NCH + 1):
                if c < NCH:
                    i = c % 2
                    act.wait_ge(rotated, c + 1)
                    if c >= 2:
                        act.wait_ge(stored[i][0], 16 * 2 * (c // 2))
                    nc.scalar.copy(parts[:, i, 0, :, :], rem[:, i, 0, :, :]).then_inc(part_done, 1)
                if c == NCH:
                    for k in range(NT // 4):
                        act.wait_ge(v_done, k + 1)
                        nc.scalar.copy(v_sb[:, 4 * k:4 * k + 4, :],
                                       banks[:, k, :].rearrange("p (t n) -> p t n", t=4)).then_inc(v_read, 1)
                if c >= 1:
                    i = (c - 1) % 2
                    act.wait_ge(rem_done, c)
                    if c >= 3:
                        act.wait_ge(stored[i][1], 16 * 2 * ((c - 1) // 2))
                    nc.scalar.copy(parts[:, i, 1, :, :], rem[:, i, 1, :, :]).then_inc(part_done, 1)
            def visit(e, r, at):
                if e[0] == "QK":
                    i = e[1]
                    n = B_STEPS[i // 2 % NB][3]
                    act.wait_ge(qk_done, at(i + 1, 2 * NB * NG))
                    if i // 2 >= 3:
                        act.wait_ge(pv_done, at(i // 2 - 2, NB * NG))
                    nc.scalar.activation(probs[i % 6][:, :, 0:n], score[:, i % 2, :, 0:n], ACT.Exp,
                                         scale=SCALE).then_inc(exp_done, 1)
                elif e[0] == "EV":
                    n = e[1]
                    act.wait_ge(pv_done, at(n // 2 * NB + C_LAST[n % 2] + 1, NB * NG))
                    if n >= 2:
                        act.wait_ge(ring_full, at(RING_OF[("OT", n - 2)] + 1, RING_BATCH))
                    nc.scalar.copy(ot[:, n % 2, :], pv[:, :]).then_inc(ot_ready, 1)
                elif e[0] == "XC":
                    bt = e[1]
                    act.wait_ge(x1_done, at(2 * bt + 2, 2))
                    nc.scalar.copy(xr[:, :, 1, 0:D], xr[:, :, 0, 0:D]).then_inc(x1_copied, 1)
                    nc.scalar.copy(x_sb[:, bass.ds(at(bt * BT, BT), BT), :], xr[:, :, 0, 0:D]).then_inc(x1_copied, 1)
                elif e[0] == "RX":
                    act.wait_ge(top_in, at(e[1] + 1, 1))
                    nc.scalar.activation(rt[:, 1, :, :], rt[:, 0, :, :], ACT.Exp).then_inc(top_exp, 1)

            walk(act, visit)

            def stage_tx(turn, k):
                act.wait_ge(xg_turned, turn * TL + (k + 1))
                if not first_use(turn, k):
                    act.wait_ge(h_done, turn * TL + (k - 1))
                nc.scalar.copy(xgT[:, k % 2, :], banks[:, k % 2, 0:P]).then_inc(xgT_ready, 1)

            def stage_gelu(turn, k):
                act.wait_ge(hb_ready, turn * TL + (k + 1))
                if not first_use(turn, k):
                    act.wait_ge(y_done, turn * TL + (k - 1))
                nc.scalar.activation(hg[:, k % 2, :], hb[:, k % 2, :], ACT.Gelu_apprx_tanh).then_inc(gelu_done, 1)

            def stage_w1(turn, k):
                e = act.value_load(expert[0:1, bass.ds(turn * TL + k, 1)], min_val=0, max_val=E - 1)
                if not first_use(turn, k):
                    act.wait_ge(h_done, turn * TL + (k - 1))
                nc.scalar.copy(w1e[:, k % 2, :], w1_sb[:, bass.ds(e, 1), :].rearrange("p a n -> p (a n)")
                               ).then_inc(w1e_ready, 1)

            act.wait_ge(tiles_ready, 1)
            act.wait_ge(late_in, 32)
            pipeline(act, ((stage_tx, 2), (stage_gelu, 1), (stage_w1, 3)))

            for t in range(NT - BT):
                if t % (2 * BT) == 0:
                    act.wait_ge(scales_ready, t // (2 * BT) + 1)
                ins = nc.scalar.activation(x_sb[:, t, :], x_sb[:, t, :], ACT.Identity, bias=shift_all[:, t:t + 1],
                                           scale=rstd_all[:, t:t + 1])
                if t % BT == BT - 1:
                    ins.then_inc(fin_ready, 1)


        @block.vector
        def _(ve):
            v = nc.vector
            link = [0]

            def chain(ins):
                link[0] += 1
                ins.then_inc(dve, 1)
                ve.wait_ge(dve, link[0])

            v.memset(region[:, 0:8192], 0.0).then_inc(stacks_clear, 1)
            ve.wait_ge(weights_in, 32)
            for c in range(NCH):
                i = c % 2
                h = c % 2
                bank = 4 * i
                ve.wait_ge(proj_done, c + 1)
                if c >= 2:
                    ve.wait_ge(rem_done, c - 1)
                cos = cs_sb[:, 0, h * CH:(h + 1) * CH].unsqueeze(1).broadcast_to([P, 2, CH])
                sin = cs_sb[:, 1, h * CH:(h + 1) * CH].unsqueeze(1).broadcast_to([P, 2, CH])
                v.tensor_tensor(rot[:, i, 0, :, :], banks[:, bank:bank + 2, :], cos, ALU.mult).then_inc(dve, 1)
                link[0] += 1
                v.tensor_tensor(rot[:, i, 1, :, :], banks[:, bank + 2:bank + 4, :], sin,
                                ALU.mult).then_inc(proj_read, 1)
                ve.wait_ge(dve, link[0])
                ve.wait_ge(proj_read, c + 1)
                v.tensor_tensor(rem[:, i, 0, :, :], rot[:, i, 0, :, :], rot[:, i, 1, :, :],
                                ALU.add).then_inc(rotated, 1)
            ve.wait_ge(loads, 16 * N_LOADS)
            v.tensor_copy(idb_sb[:, :], id_sb[:, :]).then_inc(masks_ready, 1)
            v.tensor_copy(mask_sb[:, :, :], mask_f[:, :].unsqueeze(1).broadcast_to([P, 2, P])
                          ).then_inc(masks_ready, 1)
            ve.wait_ge(v_done, NT // 4)
            v.memset(xr[:, :, :, D + 2:ROW], 0.0).then_inc(route, 1)
            v.tensor_copy(next_row[:, :], first_row_sb[:, :]).then_inc(route, 1)

            def moments(st, mean_, dev_, step, sync):
                d, m2 = dev_[:, 1, :], dev_[:, 2, :]
                step(v.tensor_tensor(mean_, st[:, :, 1], st[:, :, 4], ALU.add))
                step(v.tensor_tensor(d, st[:, :, 1], st[:, :, 4], ALU.subtract))
                step(v.tensor_tensor(m2, st[:, :, 2], st[:, :, 5], ALU.add))
                sync()
                step(v.tensor_scalar(mean_, mean_, 0.5, None, ALU.mult))
                step(v.tensor_tensor(d, d, d, ALU.mult))
                sync()
                step(v.scalar_tensor_tensor(dev_[:, 0, :], d, D / 4.0, m2, ALU.mult, ALU.add))
                sync()

            def root_start(y, var, step, sync):
                i32 = mybir.dt.int32
                step(v.tensor_scalar(y.bitcast(i32), var.bitcast(i32), 1, None, ALU.arith_shift_right))
                sync()
                step(v.tensor_scalar(y.bitcast(i32), y.bitcast(i32), -1.0, float(0x5f3759df), ALU.mult, ALU.add))
                sync()

            def root_step(y, var, t, step, sync):
                step(v.tensor_tensor(t, y, y, ALU.mult))
                sync()
                step(v.scalar_tensor_tensor(t, t, -0.5, var, ALU.mult, ALU.mult))
                sync()
                step(v.scalar_tensor_tensor(y, t, 1.5, y, ALU.add, ALU.mult))
                sync()

            bc = lambda a: a.unsqueeze(2).broadcast_to([P, BT, E])
            ib = iota_e[:, :].unsqueeze(1).broadcast_to([P, BT, E])

            def softmax(chain):
                chain(v.tensor_reduce(r1[:, 1, :], rt[:, 1, :, :], AX.X, ALU.add))
                chain(v.reciprocal(r1[:, 2, :], r1[:, 1, :]))
                chain(v.tensor_tensor(rt[:, 2, :, :], rt[:, 1, :, :], bc(r1[:, 2, :]), ALU.mult))

            def choose(r, half, chain):
                src, top = rt[:, 2 + r, :, :], r1[:, 3 + 3 * r, :]
                if half == 0:
                    if r == 0:
                        ve.wait_ge(iota_done, E + 3)
                    chain(v.tensor_reduce(top, src, AX.X, ALU.max))
                    chain(v.tensor_tensor(rt[:, 4, :, :], src, bc(top), ALU.is_equal))
                    chain(v.tensor_tensor(rt[:, 5, :, :], rt[:, 4, :, :], ib, ALU.mult))
                else:
                    chain(v.tensor_reduce(r1[:, 4, :], rt[:, 5, :, :], AX.X, ALU.min))
                    chain(v.tensor_tensor(rt[:, 6 + r, :, :], ib, bc(r1[:, 4, :]), ALU.is_equal))
                    if r == 0:
                        chain(v.scalar_tensor_tensor(rt[:, 3, :, :], rt[:, 6, :, :], -2.0, rt[:, 2, :, :],
                                                     ALU.mult, ALU.add))
                    else:
                        v.tensor_tensor(rt[:, 4, :, :], rt[:, 6, :, :], rt[:, 7, :, :], ALU.add).then_inc(top_mask, 1)

            def weigh(bt, half, chain, at):
                if half == 0:
                    chain(v.tensor_tensor(r1[:, 5, :], r1[:, 3, :], r1[:, 6, :], ALU.add))
                    chain(v.tensor_scalar(r1[:, 5, :], r1[:, 5, :], GATE_EPS, None, ALU.add))
                    chain(v.reciprocal(r1[:, 7, :], r1[:, 5, :]))
                    chain(v.tensor_tensor(xr[:, :, 0, D], r1[:, 3, :], r1[:, 7, :], ALU.mult))
                    chain(v.tensor_tensor(xr[:, :, 1, D], r1[:, 6, :], r1[:, 7, :], ALU.mult))
                else:
                    for w in range(2):
                        chain(v.tensor_copy(xr[:, :, w, D + 1], tokens_sb[:, w, bass.ds(at(bt * BT, BT), BT)]))

            def running_sums(half, chain):
                if half == 0:
                    chain(v.tensor_copy(cnt[:, 0, :, :], ranks[:, 1, :, :].rearrange("p t e -> p e t")))
                for i, sh in enumerate((1, 2, 4)):
                    if (i > 0) == half:
                        src, dst = cnt[:, i % 2, :, :], cnt[:, 1 - i % 2, :, :]
                        chain(v.tensor_copy(dst[:, :, 0:sh], src[:, :, 0:sh]))
                        chain(v.tensor_tensor(dst[:, :, sh:BT], src[:, :, sh:BT], src[:, :, 0:BT - sh], ALU.add))

            def place(half, chain):
                row = rt[:, 5, :, :]
                if half == 0:
                    chain(v.tensor_tensor(row, cnt[:, 1, :, :].rearrange("p e t -> p t e"), ranks[:, 1, :, :],
                                          ALU.subtract))
                    chain(v.tensor_tensor(row, row, ranks[:, 0, :, :], ALU.add))
                    chain(v.tensor_tensor(row, row, next_row[:, :].unsqueeze(1).broadcast_to([P, BT, E]), ALU.add))
                    chain(v.tensor_tensor(next_row[:, :], next_row[:, :], cnt[:, 1, :, BT - 1], ALU.add))
                else:
                    for w in range(2):
                        chain(v.tensor_tensor(rt[:, 8, :, :], rt[:, 6 + w, :, :], row, ALU.mult))
                        chain(v.tensor_reduce(slot_f[:, w, :], rt[:, 8, :, :], AX.X, ALU.add))
                    v.tensor_copy(slot[:, :, :], slot_f[:, :, :]).then_inc(slots_ready, 1)

            ROUTE_STEPS = {"RA": (1,), "RS": (3,), "RB": (3, 3), "RC": (3, 2), "RD": (5, 2), "RE": (3, 4), "RF": (4, 4)}
            PER_ROUTE = sum(sum(n) for n in ROUTE_STEPS.values())
            PER_LN = BT + 7 + 5 + 6

            def visit(e, r, at):
                kind = e[0]
                if r is not None:
                    bank = r % RING
                    ve.wait_ge(ring_full, at(r + 1, RING_BATCH))

                def read(ins):
                    ins.then_inc(ring_read, 1)

                if kind == "A":
                    unit, i = e[1:]
                    par, sb_, t0, n, slots, is_masked = A_ITEMS[i]
                    hs = slice(2 * slots[0] + par, 2 * slots[-1] + par + 1, 2)
                    dst = mx[:, unit % 2, hs, sb_] if t0 == 0 else mx2[:, unit % 2, hs, sb_ - BT // 2]
                    src = ring[:, bank, 0:len(slots) * n].rearrange("p (k n) -> p k n", k=len(slots))
                    read(v.tensor_reduce(dst, src, AX.X, ALU.max, negate=True))
                    if i == NA - 1:
                        ve.wait_ge(ring_read, at(r + 1, RING_BATCH))
                        v.tensor_tensor(mx[:, unit % 2, :, BT // 2:BT], mx[:, unit % 2, :, BT // 2:BT],
                                        mx2[:, unit % 2, :, :], ALU.min).then_inc(mx_ready, 1)
                elif kind == "MT":
                    read(v.tensor_copy(mparts[:, e[1] % 2, :], ring[0:GH * 3 * BT, bank, 0:P // 2].bitcast(BF16)))
                elif kind == "OT":
                    n = e[1]
                    g, c = n // 2 % NG, n % 2
                    view = ring[:, bank, :].rearrange("p (t h d) -> p t h d", t=4, h=GH)
                    inv = rden[:, c, :].rearrange("p (t h) -> p t h", t=4)
                    v.reciprocal(inv, view[:, :, :, DK]).then_inc(rden_ready, 1)
                    ve.wait_ge(rden_ready, at(n + 1, 2 * NG))
                    read(v.tensor_tensor(attn[:, c * 4:c * 4 + 4, g * 32:(g + 1) * 32].rearrange(
                                             "p t (h d) -> p t h d", h=GH),
                                         view[:, :, :, 0:DK], inv.unsqueeze(3).broadcast_to([P, 4, GH, DK]),
                                         ALU.mult))
                elif kind in ("T1", "T2"):
                    read(v.tensor_copy(aT[:, e[2], :], ring[:, bank, :]))
                elif kind == "LG":
                    read(v.tensor_tensor(logits[:, :, :],
                                         ring[:, bank, 0:BT * E].rearrange("p (t e) -> p t e", t=BT),
                                         bg_sb[:, :].unsqueeze(1).broadcast_to([P, BT, E]), ALU.add))
                elif kind == "RK":
                    read(v.tensor_copy(ranks[:, :, :, :], ring[:, bank, 0:2 * BT * E].rearrange(
                        "p (k t e) -> p k t e", k=2, t=BT)))
                elif kind in ROUTE_STEPS:
                    bt, half = e[1:]
                    order = list(ROUTE_STEPS)
                    first = 2 + bt * PER_ROUTE + sum(sum(ROUTE_STEPS[q]) for q in order[:order.index(kind)])
                    first += sum(ROUTE_STEPS[kind][:half])
                    done = [first]

                    def chain(ins):
                        ins.then_inc(route, 1)
                        done[0] += 1
                        ve.wait_ge(route, at(done[0], PER_ROUTE))

                    if kind == "RA":
                        ve.wait_ge(ring_read, at(RING_OF[("LG", bt)] + 1, RING_BATCH))
                        chain(v.tensor_reduce(r1[:, 0, :], logits[:, :, :], AX.X, ALU.max))
                        v.tensor_tensor(rt[:, 0, :, :], logits[:, :, :], bc(r1[:, 0, :]), ALU.subtract
                                        ).then_inc(top_in, 1)
                    elif kind == "RS":
                        ve.wait_ge(top_exp, at(bt + 1, 1))
                        softmax(chain)
                    elif kind == "RB":
                        choose(0, half, chain)
                    elif kind == "RC":
                        choose(1, half, chain)
                    elif kind == "RD":
                        weigh(bt, half, chain, at)
                    elif kind == "RE":
                        ve.wait_ge(ring_read, at(RING_OF[("RK", bt)] + 1, RING_BATCH))
                        running_sums(half, chain)
                    else:
                        place(half, chain)
                    assert done[0] - first == ROUTE_STEPS[kind][half], (kind, done[0] - first)
                elif kind == "WO":
                    bt, c = e[1:]
                    ve.wait_ge(x_in, 16)
                    read(v.tensor_tensor(y1[:, c, :, :], ring[:, bank, :].rearrange("p (t n) -> p t n", t=4),
                                         x_sb[:, bass.ds(at(bt * BT + 4 * c, BT), 4), :], ALU.add))
                elif kind in ("LNM", "LNV", "LNR"):
                    bt, half = e[1:]
                    done = [bt * PER_LN + {"LNM": half * BT // 2, "LNV": BT, "LNR": BT + 7 + half * 5}[kind]]

                    def step(ins):
                        ins.then_inc(ln, 1)
                        done[0] += 1

                    sync = lambda: ve.wait_ge(ln, at(done[0], PER_LN))
                    if kind == "LNM":
                        ve.wait_ge(ring_read, at(RING_OF[("WO", bt, half)] + 1, RING_BATCH))
                        for t in range(4):
                            step(v.bn_stats(stats[:, 4 * half + t, :], y1[:, half, t, :]))
                    elif kind == "LNV":
                        sync()
                        moments(stats[:, :, :], mean[:, :], dev[:, :, :], step, sync)
                        step(v.tensor_scalar(dev[:, 1, :], dev[:, 0, :], 1.0 / D, EPS, ALU.mult, ALU.add))
                    else:
                        sync()
                        if half == 0:
                            root_start(rstd[:, :], dev[:, 1, :], step, sync)
                        for _ in range(1 + half):
                            root_step(rstd[:, :], dev[:, 1, :], nwt[:, :], step, sync)
                    if kind == "LNR" and half == 1:
                        assert done[0] == (bt + 1) * PER_LN
                elif kind == "LNA":
                    bt, c = e[1:]
                    if c == 0:
                        ve.wait_ge(xr_free, at(bt + 1, 1))
                    for t in range(4):
                        k = 4 * c + t
                        last = v.tensor_scalar(xr[:, k, 0, 0:D], y1[:, c, t, :], mean[:, k:k + 1],
                                               rstd[:, k:k + 1], ALU.subtract, ALU.mult)
                    last.then_inc(x1_done, 1)

            walk(ve, visit)

            ve.wait_ge(route, 2 + B * PER_ROUTE)
            v.tensor_copy(pad_row[:, :], next_row[:, :]).then_inc(pad_ready, 1)
            chain(v.tensor_tensor(small[:, 5, :], next_row[:, :], first_row_sb[:, :], ALU.subtract))
            more = ends[:, 0:NT, :].rearrange("p t e -> p e t")
            chain(v.tensor_tensor(more, small[:, 5, :].unsqueeze(2).broadcast_to([P, E, NT]),
                                  tile128_sb[:, :].unsqueeze(1).broadcast_to([P, E, NT]), ALU.is_gt))
            chain(v.tensor_reduce(small[:, 0, :], more, AX.X, ALU.add))
            for i, sh in enumerate((1, 2, 4)):
                src, dst = small[:, i, :], small[:, i + 1, :]
                chain(v.tensor_copy(dst[:, 0:sh], src[:, 0:sh]))
                chain(v.tensor_tensor(dst[:, sh:E], src[:, sh:E], src[:, 0:E - sh], ALU.add))
            chain(v.tensor_scalar(small[:, 4, :], small[:, 0, :], -1.0, float(CAPT), ALU.mult, ALU.add))
            chain(v.tensor_tensor(ends[:, :, :], tiles_sb[:, :].unsqueeze(2).broadcast_to([P, NTILE, E]),
                                  small[:, 3, :].unsqueeze(1).broadcast_to([P, NTILE, E]), ALU.is_ge))
            chain(v.tensor_reduce(expert_f[:, 0, :], ends[:, :, :], AX.X, ALU.add))
            chain(v.tensor_scalar(expert[:, :], expert_f[:, 0, :], float(E - 1), None, ALU.min))
            chain(v.tensor_tensor(ends[:, :, :], ends[:, :, :],
                                  small[:, 4, :].unsqueeze(1).broadcast_to([P, NTILE, E]), ALU.mult))
            chain(v.tensor_reduce(expert_f[:, 1, :], ends[:, :, :], AX.X, ALU.add))
            v.tensor_tensor(tile_at[:, :], expert_f[:, 1, :], tiles_sb[:, :], ALU.add).then_inc(tiles_ready, 1)

            def stage_b1(turn, k):
                e = ve.value_load(expert[0:1, bass.ds(turn * TL + k, 1)], min_val=0, max_val=E - 1)
                ve.wait_ge(h_done, turn * TL + (k + 1))
                if not first_use(turn, k):
                    ve.wait_ge(gelu_done, turn * TL + (k - 1))
                by_chunk = lambda a: a.rearrange("p (c n) -> p c n", c=HC)
                v.tensor_tensor(by_chunk(hb[:, k % 2, :]), by_chunk(banks[:, 2 + k % 2, :]),
                                b1_sb[:, bass.ds(e, 1), :].rearrange("p a c -> p (a c)").unsqueeze(2).broadcast_to(
                                    [P, HC, P]), ALU.add).then_inc(hb_ready, 1)

            def stage_y(turn, k):
                e = ve.value_load(expert[0:1, bass.ds(turn * TL + k, 1)], min_val=0, max_val=E - 1)
                ve.wait_ge(y_done, turn * TL + (k + 1))
                v.tensor_tensor(yb[:, k % 2, :], banks[:, 6 + k % 2, 0:D],
                                b2_sb[:, bass.ds(e, 1), :].rearrange("p a n -> p (a n)"), ALU.add).then_inc(y_read, 1)
                if not (isinstance(turn, int) and turn == 0):
                    ve.wait_ge(result_out[k], turn * 16)
                v.tensor_copy(dest[:, k, :], xg[:, k, D + 1:D + 2])
                ve.wait_ge(y_read, turn * TL + (k + 1))
                v.tensor_scalar(ys[:, k, :], yb[:, k % 2, :], xg[:, k, D:D + 1], None, ALU.mult).then_inc(ys_ready, 1)

            pipeline(ve, ((stage_y, 0), (stage_b1, 2)))

            ve.wait_ge(dve, link[0])

            def step6(ins):
                link[0] += 1
                ins.then_inc(dve, 1)

            sync6 = lambda: ve.wait_ge(dve, link[0])
            for half in range(2):
                ts = slice(half * BT * 2, (half + 1) * BT * 2)
                for b in (2 * half, 2 * half + 1):
                    mine = slice(b * BT, (b + 1) * BT)
                    ve.wait_ge(first_added, b + 1)
                    chain(v.tensor_tensor(x_sb[:, mine, :], x_sb[:, mine, :], back[b][:, 1, :, :], ALU.add))
                    for t in range(b * BT, (b + 1) * BT):
                        step6(v.bn_stats(stats_all[:, t, :], x_sb[:, t, :]))
                sync6()
                mean_, dev_, rstd_ = mean_all[:, ts], dev_all[:, :, ts], rstd_all[:, ts]
                moments(stats_all[:, ts, :], mean_, dev_, step6, sync6)
                step6(v.tensor_scalar(dev_[:, 1, :], dev_[:, 0, :], 1.0 / D, EPS, ALU.mult, ALU.add))
                sync6()
                root_start(rstd_, dev_[:, 1, :], step6, sync6)
                for _ in range(3):
                    root_step(rstd_, dev_[:, 1, :], dev_[:, 2, :], step6, sync6)
                v.scalar_tensor_tensor(shift_all[:, ts], mean_, -1.0, rstd_, ALU.mult, ALU.mult
                                       ).then_inc(scales_ready, 1)
                if half == 1:
                    for t in range(NT - BT, NT):
                        ins = v.tensor_scalar(x_sb[:, t, :], x_sb[:, t, :], mean_all[:, t:t + 1],
                                              rstd_all[:, t:t + 1], ALU.subtract, ALU.mult)
                    ins.then_inc(last_ready, 1)

        @block.gpsimd
        def _(pool):
            pp = nc.gpsimd
            pp.memset(fill[:, 0, :], 0.0).then_inc(fill_set, 1)
            pp.memset(fill[:, 1, :], 1.0).then_inc(fill_set, 1)
            pp.memset(pad[:, :], 0.0).then_inc(iota_done, 1)
            pool.wait_ge(iota_done, 1)
            pp.memset(pad[:, D:D + 1], 0.0).then_inc(iota_done, 1)
            pp.memset(pad[:, D + 1:D + 2], NOWHERE).then_inc(iota_done, 1)
            for e in range(E):
                pp.memset(iota_e[:, e:e + 1], float(e - E)).then_inc(iota_done, 1)
            pp.memset(vx[:, :, :, :, :], 0.0).then_inc(vx_set, 1)
            pool.wait_ge(vx_set, 1)
            pp.memset(vx[:, :, :, :, DK:DK + 1], 1.0).then_inc(vx_set, 1)
            pp.memset(zero[:, :, :], 0.0).then_inc(vx_set, 1)
            for c in range(NCH + 1):
                if c < NCH:
                    i = c % 2
                    if c >= 2:
                        pool.wait_ge(last_done, c - 1)
                    pool.wait_ge(part_done, first_part(c))
                    pp.tensor_tensor(rem[:, i, 1, :, :], rem[:, i, 0, :, :], parts[:, i, 0, :, :],
                                     ALU.subtract).then_inc(rem_done, 1)
                if c >= 1:
                    i = (c - 1) % 2
                    pool.wait_ge(part_done, second_part(c - 1))
                    if c >= 3:
                        pool.wait_ge(stored[i][2], 16 * 2 * ((c - 1) // 2))
                    pp.tensor_tensor(parts[:, i, 2, :, :], rem[:, i, 1, :, :], parts[:, i, 1, :, :],
                                     ALU.subtract).then_inc(last_done, 1)
            pool.wait_ge(v_read, NT // 4)

            def visit(e, r, at):
                if e[0] == "VX":
                    unit = e[1]
                    if unit >= NG:
                        pool.wait_ge(pv_done, at(NB * (unit - 3), NB * NG))
                    pool.wait_ge(vx_set, 3)
                    pp.tensor_copy(vx[:, unit % NG, :, :, 0:DK],
                                   v_sb[:, bass.ds(at(unit // NG * BT, BT), BT),
                                        unit % NG * 32:(unit % NG + 1) * 32].rearrange("p t (h d) -> p t h d", h=GH)
                                   ).then_inc(vx_ready, 1)
                elif e[0] == "SPLIT":
                    unit = e[1]
                    pool.wait_ge(mx_ready, at(unit + 1, NG))
                    by_parity = lambda a: a.rearrange("p (s a) n -> p a s n", a=2)
                    neg, rest = by_parity(mx[:, unit % 2, :, :]), by_parity(mrem[:, unit % 2, :, :])
                    none = by_parity(zero[:, :, :])
                    part = [msp[:, unit % 2, :, j, :, :] for j in range(3)]
                    pp.tensor_tensor(part[0], neg, none, ALU.add).then_inc(msplit, 1)
                    pool.wait_ge(msplit, at(unit * 4 + 1, 4 * NG))
                    pp.tensor_tensor(rest, neg, part[0], ALU.subtract).then_inc(msplit, 1)
                    pool.wait_ge(msplit, at(unit * 4 + 2, 4 * NG))
                    pp.tensor_tensor(part[1], rest, none, ALU.add).then_inc(msplit, 1)
                    pool.wait_ge(msplit, at(unit * 4 + 3, 4 * NG))
                    pp.tensor_tensor(part[2], rest, part[1], ALU.subtract).then_inc(msplit, 1)
                elif e[0] == "SC":
                    bt, i = e[1:]
                    if i == 0:
                        pool.wait_ge(x1_copied, at(2 * bt + 2, 2))
                        pool.wait_ge(slots_ready, at(bt + 1, 1))
                        pool.sem_inc(pool_turns, 1)
                    t, w_ = divmod(i, 2)
                    pp.indirect_dma_start(out=pairs, out_offset=bass.IndirectOffsetOnAxis(
                                              ap=slot[:, w_, t:t + 1], axis=0),
                                          in_=xr[:, t, w_, :], in_offset=None).then_inc(pairs_out, 16)
                elif e[0] == "QK" and diagonal(e[1] // 2 % NB):
                    i = e[1]
                    pool.wait_ge(exp_done, at(i + 1, 2 * NB * NG))
                    pool.sem_inc(pool_turns, 1)
                    block_ = probs[i % 6][:, :, 0:P]
                    pp.affine_select(out=block_, in_=block_, compare_op=ALU.is_ge, fill=0.0, base=0,
                                     pattern=[[0, 2], [1, P]], channel_multiplier=-1).then_inc(masked, 1)

            walk(pool, visit)

            bound = pool.to_reg(2 * B * S - 1)

            def stage_out(turn, k):
                pool.wait_ge(ys_ready, turn * TL + (k + 1))
                pool.sem_inc(pool_turns, 1)
                pp.indirect_dma_start(out=results, out_offset=bass.IndirectOffsetOnAxis(ap=dest[:, k, :], axis=0),
                                      in_=ys[:, k, :], in_offset=None, bounds_check=bound,
                                      oob_is_err=False).then_inc(result_out[k], 16)

            pipeline(pool, ((stage_out, 0),))

            for b in range(B):
                pool.wait_ge(back_in[b], 32)
                mine = x_sb[:, b * BT:(b + 1) * BT, :]
                pp.tensor_tensor(mine, mine, back[b][:, 0, :, :], ALU.add).then_inc(first_added, 1)


def first_use(turn, k):
    return isinstance(turn, int) and turn == 0 and k < 2


def pipeline(eng, stages):
    lead = max(n for _, n in stages)
    turns = NTILE // TL
    for t in range(-lead, 0):
        for stage, n in stages:
            if 0 <= t + n:
                stage(0, t + n)
    def whole(turn):
        for k in range(TL):
            for stage, n in stages:
                stage(turn + (k + n) // TL, (k + n) % TL)

    whole(0)
    with eng.Fori(1, turns - 1) as turn:
        whole(turn)
    for k in range(TL):
        for stage, n in stages:
            if k + n < TL:
                stage(turns - 1, k + n)


def kernel(L0_attn_x, L0_attn_W_Q, L0_attn_W_K, L0_attn_W_V, L0_attn_W_O, L0_ffn_Wg, L0_ffn_bg,
           L0_ffn_W1, L0_ffn_b1, L0_ffn_W2, L0_ffn_b2):
    import concourse.bacc as bacc
    from concourse.bass_utils import run_bass_kernel_spmd

    f = lambda a: np.asarray(a)
    x = f(L0_attn_x).reshape(B * S, D)
    flip = np.arange(D).reshape(H, 2, DK // 2)[:, ::-1].reshape(-1)
    WQ, WK = f(L0_attn_W_Q), f(L0_attn_W_K)
    theta = (np.float32(1.0) / np.float32(10000.0) ** (np.arange(0, DK, 2, dtype=np.float32) / np.float32(DK)))
    ang = np.outer(np.arange(S, dtype=np.float32), theta.astype(np.float32)).astype(np.float32)
    ang = np.concatenate([ang, ang], axis=-1)
    sign = np.where(np.arange(DK) < DK // 2, -1.0, 1.0).astype(np.float32)
    cosT = np.tile(np.cos(ang).T, (H, 1)).astype(np.float32)
    sinT = np.tile((np.sin(ang) * sign).T, (H, 1)).astype(np.float32)
    q, k = np.arange(P)[:, None], np.arange(P)[None, :]
    mask_a = np.where(k > q, np.float32(-1e30), np.float32(0.0))
    arrays = {
        "xT": x.T, "x": x,
        "w": np.stack([WQ.T, WQ[flip].T, WK.T, WK[flip].T, f(L0_attn_W_V).T, f(L0_attn_W_O).T], axis=1),
        "wg": f(L0_ffn_Wg), "bg": f(L0_ffn_bg),
        "w1": f(L0_ffn_W1), "b1": f(L0_ffn_b1).reshape(E, HC, P).transpose(2, 0, 1),
        "w2": f(L0_ffn_W2), "b2": f(L0_ffn_b2),
        "cs": np.stack([cosT, sinT], axis=1), "ident": np.eye(P, dtype=np.float32),
        "maskA": mask_a,
        "before": np.stack([q < k, np.ones((P, P))], axis=1).astype(np.float32),
        "tile128": np.tile(np.arange(NT, dtype=np.float32) * P, (P, 1)),
        "tokens": np.stack([q + P * np.arange(NT), q + P * np.arange(NT) + B * S], axis=1).astype(np.float32),
        "first_row": np.tile(np.arange(E, dtype=np.float32) * (CAPT * P), (P, 1)),
        "tiles": np.tile(np.arange(NTILE, dtype=np.float32), (P, 1)),
    }
    arrays = {n: np.ascontiguousarray(a) for n, a in arrays.items()}
    nc = bacc.Bacc("TRN2", target_bir_lowering=False, num_devices=1)
    args = {n: nc.dram_tensor(f"in_{n}", a.shape, mybir.dt.from_np(a.dtype), kind="ExternalInput").ap()
            for n, a in arrays.items()}
    out = nc.dram_tensor("out_0", (B * S, D), F32, kind="ExternalOutput").ap()
    build(nc, out=out, **args)
    r = run_bass_kernel_spmd(nc, [{f"in_{n}": a for n, a in arrays.items()}], core_ids=[0])
    return r.results[0]["out_0"].reshape(B, S, D)
```
